# Optimizing a Trainium2 kernel written in Bass

```python
import numpy as np
import jax
import jax.numpy as jnp

def _softmax(x, axis=-1):
    return jax.nn.softmax(x, axis=axis)

def _gelu(x):
    return jax.nn.gelu(x, approximate=True)

def _silu(x):
    return jax.nn.silu(x)

def _sigmoid(x):
    return jax.nn.sigmoid(x)

def _layernorm(x, axis=-1, eps=1e-05):
    m = jnp.mean(x, axis=axis, keepdims=True)
    v = jnp.var(x, axis=axis, keepdims=True)
    return (x - m) / jnp.sqrt(v + eps)

def _scatter_add(tgt, idx, src, axis=0):
    return tgt.at[idx].add(src)

def _segment_sum(src, seg, n):
    return jax.ops.segment_sum(src, seg, n)
kernel_name = 'mk_recurrent_d1_jaxref_r8_343409'

def setup_inputs(seed: int=0):
    np.random.seed(seed)
    _w = jnp.asarray

    def _L0_attn_setup():
        import jax, jax.numpy as jnp
        import numpy as np
        D_MODEL, N_HEADS, N_KV, HEAD_DIM, D_LAT = (128, 8, 2, 128, 32)
        N_REP = N_HEADS // N_KV
        B, T = (2, 256)
        key = jax.random.key(seed)
        ks = jax.random.split(key, 8)
        s = lambda fan_in: 1.0 / np.sqrt(fan_in)
        return {'x': jax.random.normal(ks[0], (B, T, D_MODEL), jnp.float32), 'wq': jax.random.normal(ks[1], (D_MODEL, N_HEADS * HEAD_DIM), jnp.float32) * s(D_MODEL), 'wk_down': jax.random.normal(ks[2], (D_MODEL, N_KV * D_LAT), jnp.float32) * s(D_MODEL), 'wv_down': jax.random.normal(ks[3], (D_MODEL, N_KV * D_LAT), jnp.float32) * s(D_MODEL), 'wk_up': jax.random.normal(ks[4], (D_LAT, HEAD_DIM), jnp.float32) * s(D_LAT), 'wv_up': jax.random.normal(ks[5], (D_LAT, HEAD_DIM), jnp.float32) * s(D_LAT), 'wo': jax.random.normal(ks[6], (N_HEADS * HEAD_DIM, D_MODEL), jnp.float32) * s(N_HEADS * HEAD_DIM)}
    _L0_attn_in = _L0_attn_setup()

    def _L0_ffn_setup():
        import jax, jax.numpy as jnp
        import numpy as np
        B, S, H = (8, 512, 128)
        NAV = 128
        E = 8
        F = 2 * H
        key = jax.random.key(seed)
        ks = jax.random.split(key, 12)

        def w(k, shape, fan_in):
            return jax.random.normal(k, shape, dtype=jnp.float32) / np.sqrt(fan_in)
        return {'hidden_states': jax.random.normal(ks[0], (B, S, H), dtype=jnp.float32), 'Wp1': w(ks[1], (H, NAV), H), 'bp1': jnp.zeros((NAV,), jnp.float32), 'Wp2': w(ks[2], (NAV, E), NAV), 'bp2': jnp.zeros((E,), jnp.float32), 'W1': w(ks[3], (E, H, F), H), 'b1': jnp.zeros((E, F), jnp.float32), 'W2': w(ks[4], (E, F, H), F), 'b2': jnp.zeros((E, H), jnp.float32), 'Wo': w(ks[5], (H, H), H), 'bo': jnp.zeros((H,), jnp.float32)}
    _L0_ffn_in = _L0_ffn_setup()
    _d = {'L0_attn_x': _L0_attn_in['x'], 'L0_attn_wq': _L0_attn_in['wq'], 'L0_attn_wk_down': _L0_attn_in['wk_down'], 'L0_attn_wv_down': _L0_attn_in['wv_down'], 'L0_attn_wk_up': _L0_attn_in['wk_up'], 'L0_attn_wv_up': _L0_attn_in['wv_up'], 'L0_attn_wo': _L0_attn_in['wo'], 'L0_ffn_Wp1': _L0_ffn_in['Wp1'], 'L0_ffn_bp1': _L0_ffn_in['bp1'], 'L0_ffn_Wp2': _L0_ffn_in['Wp2'], 'L0_ffn_bp2': _L0_ffn_in['bp2'], 'L0_ffn_W1': _L0_ffn_in['W1'], 'L0_ffn_b1': _L0_ffn_in['b1'], 'L0_ffn_W2': _L0_ffn_in['W2'], 'L0_ffn_b2': _L0_ffn_in['b2'], 'L0_ffn_Wo': _L0_ffn_in['Wo'], 'L0_ffn_bo': _L0_ffn_in['bo']}
    _x0 = _d['L0_attn_x']
    _d['L0_attn_x'] = jax.random.normal(jax.random.fold_in(jax.random.key(seed), 1), (32, 256, 128), dtype=_x0.dtype)
    del _x0
    return _d

def reference(L0_attn_x, L0_attn_wq, L0_attn_wk_down, L0_attn_wv_down, L0_attn_wk_up, L0_attn_wv_up, L0_attn_wo, L0_ffn_Wp1, L0_ffn_bp1, L0_ffn_Wp2, L0_ffn_bp2, L0_ffn_W1, L0_ffn_b1, L0_ffn_W2, L0_ffn_b2, L0_ffn_Wo, L0_ffn_bo):

    def _L0_attn_ref(x, wq, wk_down, wv_down, wk_up, wv_up, wo):
        import jax, jax.numpy as jnp
        import numpy as np
        D_MODEL, N_HEADS, N_KV, HEAD_DIM, D_LAT = (128, 8, 2, 128, 32)
        N_REP = N_HEADS // N_KV
        B, T = (2, 256)
        Bq, Tq, _ = x.shape
        scale = HEAD_DIM ** (-0.5)
        q = (x @ wq).reshape(Bq, Tq, N_KV, N_REP, HEAD_DIM)
        k_lat = (x @ wk_down).reshape(Bq, Tq, N_KV, D_LAT)
        v_lat = (x @ wv_down).reshape(Bq, Tq, N_KV, D_LAT)
        k = jnp.einsum('bkhl,ld->bkhd', k_lat, wk_up)
        v = jnp.einsum('bkhl,ld->bkhd', v_lat, wv_up)
        scores = jnp.einsum('bqhrd,bkhd->bhrqk', q, k) * scale
        causal = jnp.tril(jnp.ones((Tq, Tq), dtype=bool))
        scores = jnp.where(causal, scores, jnp.finfo(scores.dtype).min)
        probs = jax.nn.softmax(scores, axis=-1)
        y = jnp.einsum('bhrqk,bkhd->bqhrd', probs, v)
        y = y.reshape(Bq, Tq, N_HEADS * HEAD_DIM)
        return y @ wo

    def _L0_ffn_ref(hidden_states, Wp1, bp1, Wp2, bp2, W1, b1, W2, b2, Wo, bo):
        import jax, jax.numpy as jnp
        import numpy as np
        B, S, H = (8, 512, 128)
        NAV = 128
        E = 8
        F = 2 * H
        last = hidden_states[:, -1, :]
        logits = jax.nn.gelu(last @ Wp1 + bp1, approximate=False) @ Wp2 + bp2
        action_probs = jax.nn.softmax(logits, axis=-1)
        sel = jnp.argmax(action_probs, axis=-1)
        w1 = W1[sel]
        w2 = W2[sel]
        h = jax.nn.gelu(jnp.einsum('bsh,bhf->bsf', hidden_states, w1) + b1[sel][:, None, :], approximate=False)
        reasoned = jnp.einsum('bsf,bfh->bsh', h, w2) + b2[sel][:, None, :]
        out = reasoned @ Wo + bo
        return hidden_states + 0.3 * out
    x = L0_attn_x
    xn = _layernorm(x, axis=-1)
    s = _L0_attn_ref(xn, L0_attn_wq, L0_attn_wk_down, L0_attn_wv_down, L0_attn_wk_up, L0_attn_wv_up, L0_attn_wo)
    g = _silu(_L0_ffn_ref(xn, L0_ffn_Wp1, L0_ffn_bp1, L0_ffn_Wp2, L0_ffn_bp2, L0_ffn_W1, L0_ffn_b1, L0_ffn_W2, L0_ffn_b2, L0_ffn_Wo, L0_ffn_bo))
    x = x + s * g
    return x

_drawn_inputs = setup_inputs


def setup_inputs(seed=0):
    import zlib

    import numpy as np

    out = dict(_drawn_inputs(seed))
    spreads = {'L0_ffn_bp1': (0.0, 0.778),
     'L0_ffn_bp2': (0.0, 0.504),
     'L0_ffn_b1': (0.0, 2.0),
     'L0_ffn_b2': (0.0, 0.8),
     'L0_ffn_bo': (0.0, 0.8)}
    factors = {}
    for name, (base, spread) in spreads.items():
        noise = np.random.default_rng([zlib.crc32(name.encode()), seed]).standard_normal(out[name].shape)
        drawn = base * np.exp(spread * noise) if base else spread * noise
        out[name] = jnp.asarray(drawn.astype(out[name].dtype))
    for name, factor in factors.items():
        out[name] = (out[name] * factor).astype(out[name].dtype)
    return out
```

```python
import concourse.bass as bass
from concourse import mybir
from contextlib import ExitStack
import numpy as np


def layernorm_mla_attention_times_routed_ffn_gate(
    nc, x, wq, wk_down, wv_down, wk_up, wv_up, wo,
    Wp1, bp1, Wp2, bp2, W1, b1, W2, b2, Wo, bo, out,
):
    f32, f32r, bf16 = mybir.dt.float32, mybir.dt.float32r, mybir.dt.bfloat16
    i32, u32 = mybir.dt.int32, mybir.dt.uint32
    ALU, ACT, AX = mybir.AluOpType, mybir.ActivationFunctionType, mybir.AxisListType

    B, T, D = x.shape
    L = wk_up.shape[0]
    G = wk_down.shape[1] // L
    HD = wk_up.shape[1]
    H = wq.shape[1] // HD
    R = H // G
    E, _, F = W1.shape
    FB, TB = F // 128, T // 128
    VW = L + 1
    SCALE = float(HD) ** -0.5
    MASKED = -1e30
    EPS = 1e-5
    W1_AT, W2O_AT, B2O_AT, B1_AT = 0, F, 2 * F, 2 * F + D
    EW = B1_AT + FB
    KR = 3 * L
    KM = KR + 2
    SU = 8
    PU = 6
    RING = 9
    CYC = 3

    ctx = ExitStack()
    with ctx:
        def sb(name, shape, dt=f32):
            return ctx.enter_context(nc.sbuf_tensor(name, shape, dt))

        def sem(name):
            return ctx.enter_context(nc.semaphore(name))

        xnT_all = sb("xnT_all", [128, B, T])
        gate_all = sb("gate_all", [128, B, TB, D])
        v_all = sb("v_all", [128, B, TB, G, VW])
        A = sb("A", [128, H * L])
        WK3 = sb("WK3", [128, G, 3, L])
        wvd = sb("wvd", [128, G * L])
        U = sb("U", [128, G, D])
        ident = sb("ident", [128, 128])
        identb = sb("identb", [128, 128], bf16)
        causal = sb("causal", [128, 2, 128], bf16)
        ones_row = sb("ones_row", [1, 128])
        neg_half = sb("neg_half", [128, TB])
        sel_row = sb("sel_row", [1, B], i32)
        big = sb("big", [128, RING * 1024])
        table = big[:, 0:E * EW].rearrange("p (e w) -> p e w", e=E)
        o = E * EW
        wsel = big[:, o:o + CYC * EW].rearrange("p (c w) -> p c w", c=CYC)
        o += CYC * EW
        hT = big[:, o:o + CYC * FB * T].rearrange("p (c f t) -> p c f t", c=CYC, f=FB)
        o += CYC * FB * T
        assert o <= RING * 1024
        probs = big[:, 0:RING * 512].rearrange("p (u n) -> p u n", u=RING)
        flat = gate_all[:, :, :, :].rearrange("p b j d -> p (b j d)")
        W2T = flat[:, 0:2048].rearrange("p (e f j) -> p e f j", e=E, f=FB)
        wqT = flat[:, 2048:3072].rearrange("p (h d) -> p h d", h=H)
        b2rep = flat[:, 3072:4096].rearrange("p (e j) -> p e j", e=E)
        flat2 = xnT_all[:, :, :].rearrange("p b t -> p (b t)")
        W2_sb = flat2[:, 0:2048].rearrange("p (e f h) -> p e f h", e=E, f=FB)
        wq_sb = flat2[:, 2048:3072].rearrange("p (h d) -> p h d", h=H)
        wo_sb = flat2[:, 3072:4096].rearrange("p (h d) -> p h d", h=H)
        Wo_sb = flat2[:, 4096:4224]
        wup = flat2[0:L, 4224:4480].rearrange("l (k d) -> l k d", k=2)
        b1_sb = flat2[0:E, 4480:4736]
        b2_sb = flat2[0:E, 4736:4864]
        bo_sb = flat2[0:1, 4864:4992]
        Wp1_sb = flat2[:, 4992:5120]
        Wp2_sb = flat2[:, 5120:5128]
        bp1_sb = flat2[:, 5128:5129]
        bp2_sb = flat2[0:1, 5136:5144]
        wkd_sb = flat2[:, 5144:5208].rearrange("p (g l) -> p g l", g=G)
        xlast = flat2[0:B, 5248:5376]
        xnlast = flat2[0:B, 5376:5504]
        lastT = flat2[:, 5504:5504 + B]
        navT = flat2[:, 5536:5536 + B]
        logits = flat2[0:B, 5568:5576]
        top8 = flat2[0:B, 5576:5584]
        wupT = flat2[:, 5600:5664].rearrange("p (k l) -> p k l", k=2)
        st_last = flat2[0:B, 5664:5670]
        mv_last = flat2[0:B, 5672:5674]
        rs_last = flat2[0:B, 5674:5675]
        selF = flat2[0:B, 5675:5676]
        sel_idx = sb("sel_idx", [B, 8], u32)
        x_in = sb("x_in", [128, CYC, TB, D])
        xn = sb("xn", [128, CYC, TB, D])
        xT = sb("xT", [128, CYC, T])
        stats = sb("stats", [128, CYC, TB, 6])
        mv = sb("mv", [128, CYC, TB, 2])
        var_eps = sb("var_eps", [128, CYC, TB])
        rstd = sb("rstd", [128, CYC, TB])
        xb = sb("xb", [128, CYC, TB, D])
        z = sb("z", [128, CYC, TB, D])
        th = sb("th", [128, CYC, TB, D])
        th1 = sb("th1", [128, CYC, TB, D])
        q_hi = sb("q_hi", [128, CYC, G, T], f32r)
        q_lo = sb("q_lo", [128, CYC, G, T], f32r)
        q_stack = sb("q_stack", [128, CYC, H, T], f32r)
        k_stack = sb("k_stack", [128, CYC, G, T], f32r)
        neg_max = sb("neg_max", [128, CYC, TB, H])
        m_hi = sb("m_hi", [H, T], f32r)
        m_lo = sb("m_lo", [H, T], f32r)
        v_w = sb("v_w", [128, CYC, TB, G, VW])
        rden = sb("rden", [128, CYC, TB, H])
        yn = sb("yn", [128, CYC, TB, H, L])
        yT = sb("yT", [128, G, T])
        sg = sb("sg", [128, CYC, TB, D])
        res = sb("res", [128, CYC, TB, D])

        bank = [ctx.enter_context(nc.psum_tensor(f"bank{i}", [128, 512], f32)) for i in range(8)]

        ld_router, ld_small, ld_wq, ld_w2 = sem("ld_router"), sem("ld_small"), sem("ld_wq"), sem("ld_w2")
        ld_wo, ld_w1 = sem("ld_wo"), sem("ld_w1")
        pool_set, pool_const = sem("pool_set"), sem("pool_const")
        dve_const = sem("dve_const")
        wk3_ready = sem("wk3_ready")
        last_step = sem("last_step")
        small_T, small_cp = sem("small_T"), sem("small_cp")
        last_T, last_cp = sem("last_T"), sem("last_cp")
        nav_ps, nav_cp = sem("nav_ps"), sem("nav_cp")
        lg_ps, sel_step = sem("lg_ps"), sem("sel_step")
        selT_ps, sel_ready = sem("selT_ps"), sem("sel_ready")
        wqT_ps, wqT_cp = sem("wqT_ps"), sem("wqT_cp")
        w2T_ps, w2T_cp = sem("w2T_ps"), sem("w2T_cp")
        A_ps, U_ps, w2o_ps, b2o_ps = sem("A_ps"), sem("U_ps"), sem("w2o_ps"), sem("b2o_ps")
        A_cp, U_cp, tab_cp = sem("A_cp"), sem("U_cp"), sem("tab_cp")
        bn_st, bn_ag = sem("bn_st"), sem("bn_ag")
        x1_ld = [sem(f"x1_ld{c}") for c in range(CYC)]
        eps_add, rstd_ok, xn_ok = sem("eps_add"), sem("rstd_ok"), sem("xn_ok")
        xT_ps, xT_ok, wsel_ok, xT_kept, xb_ok = sem("xT_ps"), sem("xT_ok"), sem("wsel_ok"), sem("xT_kept"), sem("xb_ok")
        v_ps, v_kept, h_ps, h_ok, f2_ps, z_ok = sem("v_ps"), sem("v_kept"), sem("h_ps"), sem("h_ok"), sem("f2_ps"), sem("z_ok")
        th_ok, th1_ok, gate_ok = sem("th_ok"), sem("th1_ok"), sem("gate_ok")
        k_ps, q_ps, k_hi_ok, q_hi_ok, k_lo_ok, q_lo_ok = (sem(n) for n in (
            "k_ps", "q_ps", "k_hi_ok", "q_hi_ok", "k_lo_ok", "q_lo_ok"))
        m_stacked = sem("m_stacked")
        q_stacked = [sem(f"q_stacked{c}") for c in range(CYC)]
        s_ps, max_ok, mT_ps, m_hi_ok, m_lo_ok = (sem(n) for n in ("s_ps", "max_ok", "mT_ps", "m_hi_ok", "m_lo_ok"))
        st_ps, exp_ok, causal_ok = sem("st_ps"), sem("exp_ok"), sem("causal_ok")
        vw_ok, pv_ps, rden_ok, yn_ok = sem("vw_ok"), sem("pv_ps"), sem("rden_ok"), sem("yn_ok")
        yT_ps, yT_ok, s_out, sg_ok, res_ok = (sem(n) for n in ("yT_ps", "yT_ok", "s_out", "sg_ok", "res_ok"))
        x2_ld = [sem(f"x2_ld{c}") for c in range(CYC)]
        out_st = [sem(f"out_st{c}") for c in range(CYC)]

        block = ctx.enter_context(nc.Block())

        STACK_DMAS = 3 * R * 16
        x_v = x.rearrange("b (j p) d -> b p j d", p=128)
        out_v = out.rearrange("b (j p) d -> b p j d", p=128)

        def run(eng, step, lags, first):
            last_full = B - 1
            turns = (last_full - first + 1) // CYC
            for s in range(first):
                step(s, 0, 0, False)
            with eng.Fori(0, turns) as i:
                for s in range(first, first + CYC):
                    step(s, i * CYC, i, True)
            for s in range(first + turns * CYC, B + lags):
                step(s, 0, 0, False)

        LAGS1, FIRST1 = 4, 7
        LAGS2, FIRST2 = 4, 7

        def count(eng, n, looped):
            return eng.snap(eng.to_reg(n)) if looped else n

        def live(b, looped):
            return looped or 0 <= b < B

        @block.sync
        def _(sp):
            ld = sp.dma_start
            ld(xlast, x[:, T - 1, :]).then_inc(ld_router, 16)
            ld(Wp1_sb, Wp1).then_inc(ld_router, 16)
            ld(bp1_sb, bp1.rearrange("(n o) -> n o", o=1)).then_inc(ld_router, 16)
            ld(Wp2_sb, Wp2).then_inc(ld_router, 16)
            ld(bp2_sb, bp2.rearrange("(o n) -> o n", o=1)).then_inc(ld_router, 16)
            ld(wup[:, 0, :], wk_up).then_inc(ld_small, 16)
            ld(wup[:, 1, :], wv_up).then_inc(ld_small, 16)
            ld(b1_sb, b1).then_inc(ld_small, 16)
            ld(b2_sb, b2).then_inc(ld_small, 16)
            ld(wq_sb, wq.rearrange("p (h d) -> p h d", h=H)).then_inc(ld_wq, 16)
            ld(W2_sb, W2.rearrange("e (f p) h -> p e f h", p=128)).then_inc(ld_w2, 16)
            ld(Wo_sb, Wo).then_inc(ld_wo, 16)
            ld(bo_sb, bo.rearrange("(o n) -> o n", o=1)).then_inc(ld_wo, 16)
            ld(wo_sb, wo.rearrange("(h p) o -> p h o", p=128)).then_inc(ld_wo, 16)
            ld(table[:, :, W1_AT:W1_AT + F], W1.rearrange("e p f -> p e f")).then_inc(ld_w1, 16)
            ld(wkd_sb, wk_down.rearrange("p (g l) -> p g l", g=G)).then_inc(ld_w1, 16)
            ld(wvd[:, :], wv_down).then_inc(ld_w1, 16)

            def step1(s, o, w, looped):
                b = s
                if live(b, looped):
                    c = b % CYC
                    sp.wait_ge(ld_router, 80)
                    if b >= CYC:
                        sp.wait_ge(xn_ok, b + o - CYC + 1)
                    sp.dma_start(x_in[:, c, :, :], x_v[bass.ds(b + o, 1), :, :, :].rearrange("o p j d -> p (o j) d")).then_inc(x1_ld[c], 16)

            run(sp, step1, LAGS1, FIRST1)

            def step2(s, o, w, looped):
                b = s - 4
                if live(b, looped):
                    c = b % CYC
                    sp.wait_ge(ld_router, 80)
                    if b >= CYC:
                        sp.wait_ge(res_ok, b + o - CYC + 1)
                    elif b == 0:
                        sp.wait_ge(xn_ok, B)
                    sp.dma_start(x_in[:, c, :, :], x_v[bass.ds(b + o, 1), :, :, :].rearrange("o p j d -> p (o j) d")).then_inc(x2_ld[c], 16)
                b = s
                if live(b, looped):
                    c = b % CYC
                    made = count(sp, b + o + 1, looped)
                    if b >= CYC:
                        sp.wait_ge(st_ps, PU * (b + o - CYC + 1))
                    for part, at in ((q_hi, 0), (q_hi, 2), (q_lo, 1)):
                        if at == 0:
                            sp.wait_ge(q_hi_ok, made)
                        if at == 1:
                            sp.wait_ge(q_lo_ok, made)
                        for r in range(R):
                            sp.dma_start(q_stack[at * L:at * L + L, c, r:H:R, :].bitcast(f32),
                                         part[r * L:r * L + L, c, :, :].bitcast(f32)).then_inc(q_stacked[c], 16)
                b = s - 4
                if live(b, looped):
                    c = b % CYC
                    sp.wait_ge(ld_router, 80)
                    sp.wait_ge(res_ok, b + o + 1)
                    sp.dma_start(out_v[bass.ds(b + o, 1), :, :, :].rearrange("o p j d -> p (o j) d"), res[:, c, :, :]).then_inc(out_st[c], 16)
                b = s - 1
                if live(b, looped):
                    c = b % CYC
                    sp.wait_ge(m_hi_ok, b + o + 1)
                    sp.dma_start(q_stack[KR:KR + 1, c, :, :].bitcast(f32), m_hi[:, :].bitcast(f32)).then_inc(m_stacked, 16)
                    sp.wait_ge(m_lo_ok, b + o + 1)
                    sp.dma_start(q_stack[KR + 1:KR + 2, c, :, :].bitcast(f32), m_lo[:, :].bitcast(f32)).then_inc(m_stacked, 16)

            run(sp, step2, LAGS2, FIRST2)
            for c in range(CYC):
                sp.wait_ge(out_st[c], 16 * ((B - c + CYC - 1) // CYC))

        @block.gpsimd
        def _(pool):
            nc.gpsimd.memset(ident[:, :], 0.0).then_inc(pool_set, 1)
            nc.gpsimd.memset(causal[:, :, :], 0.0).then_inc(pool_set, 1)
            nc.gpsimd.memset(neg_half[:, :], -0.5)
            pool.wait_ge(pool_set, 1)
            nc.gpsimd.affine_select(out=ident[:, :], in_=ident[:, :], compare_op=ALU.not_equal, fill=1.0,
                                    base=0, pattern=[[-1, 128]], channel_multiplier=1).then_inc(pool_const, 1)
            pool.wait_ge(pool_set, 2)
            nc.gpsimd.affine_select(out=causal[:, :, :], in_=causal[:, :, :], compare_op=ALU.is_ge, fill=MASKED,
                                    base=0, pattern=[[0, 2], [-1, 128]], channel_multiplier=1)
            pool.wait_ge(pool_const, 1)
            nc.gpsimd.tensor_copy(identb[:, :], ident[:, :]).then_inc(pool_const, 1)
            pool.wait_ge(last_step, 2)
            nc.gpsimd.tensor_scalar(rs_last, mv_last[:, 1:2], EPS, None, ALU.add).then_inc(last_step, 1)
            pool.wait_ge(last_step, 3)
            nc.gpsimd.tensor_tensor(rs_last, rs_last, neg_half[0:B, 0:1], ALU.pow).then_inc(last_step, 1)
            pool.wait_ge(ld_w1, 48)
            for r in range(3):
                last = nc.gpsimd.tensor_copy(WK3[:, :, r, :], wkd_sb)
            last.then_inc(wk3_ready, 1)

            def step1(s, o, w, looped):
                b = s
                if live(b, looped):
                    c = b % CYC
                    made = count(pool, b + o + 1, looped)
                    pool.wait_ge(pool_const, 2)
                    pool.wait_ge(bn_ag, made)
                    nc.gpsimd.tensor_scalar(var_eps[:, c, :], mv[:, c, :, 1], EPS, None, ALU.add).then_inc(eps_add, 1)
                    pool.wait_ge(eps_add, b + o + 1)
                    if b >= CYC:
                        pool.wait_ge(xn_ok, b + o - CYC + 1)
                    nc.gpsimd.tensor_tensor(rstd[:, c, :], var_eps[:, c, :], neg_half[:, :], ALU.pow).then_inc(rstd_ok, 1)
                b = s - 1
                if live(b, looped):
                    c = b % CYC
                    if b == 0:
                        pool.wait_ge(tab_cp, 7)
                        pool.wait_ge(ld_w1, 48)
                        pool.wait_ge(sel_ready, 1)
                    if b >= CYC:
                        pool.wait_ge(f2_ps, b + o - CYC + 1)
                        pool.wait_ge(h_ok, b + o - CYC + 1)
                        pool.wait_ge(xb_ok, b + o - CYC + 1)
                    expert = nc.gpsimd.value_load(sel_row[0:1, bass.ds(b + o, 1)], min_val=0, max_val=E - 1)
                    nc.gpsimd.tensor_copy(wsel[:, c, :], table[:, bass.ds(expert, 1), :].rearrange("p o w -> p (o w)")).then_inc(wsel_ok, 1)
                b = s - 2
                if live(b, looped):
                    c = b % CYC
                    pool.wait_ge(xT_ok, b + o + 1)
                    if b == 0:
                        pool.wait_ge(tab_cp, 7)
                        pool.wait_ge(A_cp, 1)
                        pool.wait_ge(U_cp, 1)
                        pool.wait_ge(wk3_ready, 1)
                    nc.gpsimd.tensor_copy(xnT_all[:, bass.ds(b + o, 1), :].rearrange("p o t -> p (o t)"), xT[:, c, :]).then_inc(xT_kept, 1)
                    pool.wait_ge(wsel_ok, b + o + 1)
                    if b >= CYC:
                        pool.wait_ge(z_ok, b + o - CYC + 1)
                    for j in range(TB):
                        last = nc.gpsimd.tensor_tensor(xb[:, c, j, :], xn[:, c, j, :], wsel[:, c, B2O_AT:B2O_AT + D], ALU.add)
                    last.then_inc(xb_ok, 1)
                b = s - 4
                if live(b, looped):
                    c = b % CYC
                    made = count(pool, b + o + 1, looped)
                    freed = count(pool, b + o - CYC + 1, looped)
                    pool.wait_ge(pool_const, 2)
                    if b >= CYC:
                        pool.wait_ge(gate_ok, freed)
                    pool.wait_ge(th_ok, made)
                    nc.gpsimd.tensor_scalar(th1[:, c, :, :], th[:, c, :, :], 1.0, None, ALU.add).then_inc(th1_ok, 1)
                    pool.wait_ge(th1_ok, b + o + 1)
                    pool.wait_ge(z_ok, b + o + 1)
                    nc.gpsimd.tensor_tensor(gate_all[:, bass.ds(b + o, 1), :, :].rearrange("p o j d -> p (o j) d"),
                                            th1[:, c, :, :], z[:, c, :, :], ALU.mult).then_inc(gate_ok, 1)

            run(pool, step1, LAGS1, FIRST1)

            def step2(s, o, w, looped):
                b = s - 2
                if live(b, looped):
                    c = b % CYC
                    if b == 0:
                        pool.wait_ge(v_kept, B)
                    if b >= CYC:
                        pool.wait_ge(pv_ps, H * TB * (b + o - CYC + 1))
                    nc.gpsimd.tensor_copy(v_w[:, c, :, :, :].rearrange("p j g w -> p (j g w)"),
                                          v_all[:, bass.ds(b + o, 1), :, :, :].rearrange("p o j g w -> p (o j g w)")).then_inc(vw_ok, 1)
                    for t in range(PU):
                        u = (PU * b + t) % RING
                        made = count(pool, PU * (b + o) + t + 1, looped)
                        pool.wait_ge(pool_const, 2)
                        pool.wait_ge(exp_ok, made)
                        if t % 3 < 2:
                            cut = probs[:, u, :].rearrange("p (h q) -> p h q", h=2)[:, :, 0:128]
                            heads = 2
                        else:
                            cut = probs[:, u, :].rearrange("p (h q) -> p h q", h=R)
                            heads = R
                        nc.gpsimd.affine_select(out=cut, in_=cut, compare_op=ALU.is_ge, fill=0.0, base=0,
                                                pattern=[[0, heads], [1, 128]], channel_multiplier=-1).then_inc(causal_ok, 1)
                b = s - 4
                if live(b, looped):
                    c = b % CYC
                    pool.wait_ge(sg_ok, b + o + 1)
                    pool.wait_ge(x2_ld[c], 16 * (b // CYC + w + 1))
                    if b >= CYC:
                        pool.wait_ge(out_st[c], 16 * (b // CYC + w))
                    nc.gpsimd.tensor_tensor(res[:, c, :, :], sg[:, c, :, :], x_in[:, c, :, :], ALU.add).then_inc(res_ok, 1)

            run(pool, step2, LAGS2, FIRST2)

        @block.scalar
        def _(act):
            act.wait_ge(nav_ps, 1)
            nc.scalar.activation(navT, bank[6][:, 0:B], ACT.Gelu, bias=bp1_sb).then_inc(nav_cp, 1)
            for i in range(4):
                act.wait_ge(w2T_ps, i + 1)
                nc.scalar.copy(flat[:, 512 * i:512 * i + 512], bank[2 + i][:, :]).then_inc(w2T_cp, 1)
            act.wait_ge(A_ps, 1)
            nc.scalar.mul(A[:, :], bank[0][:, 0:H * L], SCALE).then_inc(A_cp, 1)
            for i in range(4):
                act.wait_ge(w2o_ps, i + 1)
                nc.scalar.mul(table[:, 2 * i:2 * i + 2, W2O_AT:W2O_AT + F],
                              bank[2 + i][:, :].rearrange("p (e n) -> p e n", e=2), 0.3).then_inc(tab_cp, 1)

            def step1(s, o, w, looped):
                b = s - 2
                if live(b, looped):
                    c = b % CYC
                    if b >= CYC:
                        act.wait_ge(f2_ps, b + o - CYC + 1)
                    act.wait_ge(wsel_ok, b + o + 1)
                    act.wait_ge(h_ps, b + o + 1)
                    for f in range(FB):
                        last = nc.scalar.activation(hT[:, c, f, :], bank[2 + c][:, f * T:f * T + T], ACT.Gelu,
                                                    bias=wsel[:, c, B1_AT + f:B1_AT + f + 1])
                    last.then_inc(h_ok, 1)
                b = s - 3
                if live(b, looped):
                    c = b % CYC
                    act.wait_ge(z_ok, b + o + 1)
                    if b >= CYC:
                        act.wait_ge(th1_ok, b + o - CYC + 1)
                    nc.scalar.activation(th[:, c, :, :], z[:, c, :, :], ACT.Tanh, scale=0.5).then_inc(th_ok, 1)

            run(act, step1, LAGS1, FIRST1)

            def step2(s, o, w, looped):
                b = s
                if live(b, looped):
                    c = b % CYC
                    if b >= CYC:
                        act.wait_ge(st_ps, PU * (b + o - CYC + 1))
                        act.wait_ge(q_stacked[c], STACK_DMAS * (b // CYC + w))
                        act.wait_ge(q_lo_ok, b + o - CYC + 1)
                    act.wait_ge(k_ps, b + o + 1)
                    nc.scalar.copy(k_stack[0:KR, c, :, :], bank[1][0:KR, :].rearrange("p (g t) -> p g t", g=G)).then_inc(k_hi_ok, 1)
                    act.wait_ge(q_ps, b + o + 1)
                    nc.scalar.copy(q_hi[:, c, :, :], bank[0][:, :].rearrange("p (g t) -> p g t", g=G)).then_inc(q_hi_ok, 1)
                b4 = s - 4
                if live(b4, looped):
                    act.wait_ge(yT_ps, b4 + o + 1)
                    if b4 >= 1:
                        act.wait_ge(s_out, b4 + o)
                    nc.scalar.copy(yT[:, :, :], bank[7][:, :].rearrange("p (g t) -> p g t", g=G)).then_inc(yT_ok, 1)
                b = s - 2
                if live(b, looped):
                    if b == 0:
                        act.wait_ge(gate_ok, B)
                    for t in range(PU):
                        n = PU * b + t
                        if n >= RING:
                            if t < 3:
                                act.wait_ge(pv_ps, H * TB * (b + o - 1))
                            else:
                                act.wait_ge(pv_ps, H * TB * (b + o - 1) + H + R)
                        act.wait_ge(st_ps, PU * (b + o) + t + 1)
                        nc.scalar.activation(probs[:, n % RING, :], bank[4 + t % 2][:, :], ACT.Exp).then_inc(exp_ok, 1)
                b = s - 1
                if live(b, looped):
                    act.wait_ge(mT_ps, b + o + 1)
                    if b >= 1:
                        act.wait_ge(m_stacked, 32 * (b + o))
                        act.wait_ge(m_lo_ok, b + o)
                    nc.scalar.copy(m_hi[:, :], bank[7][0:H, 0:T]).then_inc(m_hi_ok, 1)

            run(act, step2, LAGS2, FIRST2)

        @block.vector
        def _(dve):
            nc.vector.memset(ones_row[:, :], 1.0)
            nc.vector.memset(v_all[:, :, :, :, L:VW], 1.0)
            nc.vector.memset(k_stack[KR:KM, :, :, :].bitcast(f32), 1.0).then_inc(dve_const, 1)
            dve.wait_ge(ld_router, 80)
            nc.vector.bn_stats(st_last, xlast).then_inc(last_step, 1)
            dve.wait_ge(last_step, 1)
            nc.vector.bn_aggr(mv_last, st_last).then_inc(last_step, 1)
            dve.wait_ge(last_step, 4)
            nc.vector.tensor_scalar(xnlast, xlast, mv_last[:, 0:1], rs_last, ALU.subtract, ALU.mult).then_inc(last_step, 1)
            dve.wait_ge(last_T, 1)
            nc.vector.tensor_copy(lastT, bank[6][:, 32:32 + B]).then_inc(last_cp, 1)
            dve.wait_ge(small_T, 1)
            nc.vector.tensor_copy(wupT, bank[7][:, 32:96].rearrange("p (k l) -> p k l", k=2))
            nc.vector.tensor_copy(b2rep, bank[7][:, 96:96 + E, None].to_broadcast([128, E, 128]))
            nc.vector.tensor_copy(table[:, :, B1_AT:B1_AT + FB],
                                  bank[7][:, 104:104 + E * FB].rearrange("p (f e) -> p e f", f=FB)).then_inc(tab_cp, 1)
            for i in range(2):
                dve.wait_ge(wqT_ps, i + 1)
                nc.vector.tensor_copy(wqT[:, 4 * i:4 * i + 4, :], bank[i][:, :].rearrange("p (h d) -> p h d", h=4)).then_inc(wqT_cp, 1)
            dve.wait_ge(lg_ps, 1)
            nc.vector.tensor_copy(logits, bank[6][0:B, 64:64 + E]).then_inc(sel_step, 1)
            dve.wait_ge(sel_step, 1)
            nc.vector.max(top8, logits).then_inc(sel_step, 1)
            dve.wait_ge(sel_step, 2)
            nc.vector.max_index(sel_idx[:, :], top8, logits).then_inc(sel_step, 1)
            dve.wait_ge(sel_step, 3)
            nc.vector.tensor_copy(selF, sel_idx[:, 0:1]).then_inc(sel_step, 1)
            dve.wait_ge(selT_ps, 1)
            nc.vector.tensor_copy(sel_row[:, :], bank[6][0:1, 96:96 + B]).then_inc(sel_ready, 1)
            dve.wait_ge(U_ps, 1)
            nc.vector.tensor_scalar(U[:, :, :], bank[1][:, 0:G * D].rearrange("p (g o) -> p g o", g=G), 0.5, None, ALU.mult).then_inc(U_cp, 1)
            for i in range(2):
                dve.wait_ge(b2o_ps, i + 1)
                nc.vector.tensor_scalar(table[:, 4 * i:4 * i + 4, B2O_AT:B2O_AT + D],
                                        bank[6 + i][:, :].rearrange("p (e o) -> p e o", e=4), 0.3, None, ALU.mult).then_inc(tab_cp, 1)

            def step1(s, o, w, looped):
                b = s
                if live(b, looped):
                    c = b % CYC
                    dve.wait_ge(x1_ld[c], 16 * (b // CYC + w + 1))
                    if b >= CYC:
                        dve.wait_ge(eps_add, b + o - CYC + 1)
                    made = count(dve, b + o + 1, looped)
                    for j in range(TB):
                        last = nc.vector.bn_stats(stats[:, c, j, :], x_in[:, c, j, :])
                    last.then_inc(bn_st, 1)
                    dve.wait_ge(dve_const, 1)
                    dve.wait_ge(bn_st, made)
                    for j in range(TB):
                        last = nc.vector.bn_aggr(mv[:, c, j, :], stats[:, c, j, :])
                    last.then_inc(bn_ag, 1)
                b = s - 1
                if live(b, looped):
                    c = b % CYC
                    dve.wait_ge(xT_ps, b + o + 1)
                    if b >= CYC:
                        dve.wait_ge(h_ps, b + o - CYC + 1)
                        dve.wait_ge(xT_kept, b + o - CYC + 1)
                    nc.vector.tensor_copy(xT[:, c, :], bank[0][:, 0:T]).then_inc(xT_ok, 1)
                b = s
                if live(b, looped):
                    c = b % CYC
                    dve.wait_ge(rstd_ok, b + o + 1)
                    if b >= CYC:
                        dve.wait_ge(xb_ok, b + o - CYC + 1)
                        dve.wait_ge(xT_ps, b + o - CYC + 1)
                    for j in range(TB):
                        last = nc.vector.tensor_scalar(xn[:, c, j, :], x_in[:, c, j, :], mv[:, c, j, 0:1], rstd[:, c, j:j + 1],
                                                       ALU.subtract, ALU.mult)
                    last.then_inc(xn_ok, 1)
                b = s - 2
                if live(b, looped):
                    dve.wait_ge(v_ps, b + o + 1)
                    nc.vector.tensor_copy(v_all[:, bass.ds(b + o, 1), :, :, 0:L].rearrange("p o j g l -> p (o j) g l"),
                                          bank[1][:, 0:TB * G * L].rearrange("p (j g l) -> p j g l", j=TB, g=G)).then_inc(v_kept, 1)
                b = s - 3
                if live(b, looped):
                    c = b % CYC
                    dve.wait_ge(f2_ps, b + o + 1)
                    dve.wait_ge(xb_ok, b + o + 1)
                    if b >= CYC:
                        dve.wait_ge(gate_ok, b + o - CYC + 1)
                    nc.vector.tensor_tensor(z[:, c, :, :], bank[5 + c][:, 0:TB * D].rearrange("p (j d) -> p j d", j=TB),
                                            xb[:, c, :, :], ALU.add).then_inc(z_ok, 1)

            run(dve, step1, LAGS1, FIRST1)

            def step2(s, o, w, looped):
                b = s
                if live(b, looped):
                    c = b % CYC
                    dve.wait_ge(k_hi_ok, b + o + 1)
                    rows = slice(2 * L, 3 * L)
                    nc.vector.tensor_tensor(k_stack[rows, c, :, :], bank[1][rows, :].rearrange("p (g t) -> p g t", g=G),
                                            k_stack[rows, c, :, :].bitcast(f32), ALU.subtract).then_inc(k_lo_ok, 1)
                    dve.wait_ge(q_hi_ok, b + o + 1)
                    if b >= CYC:
                        dve.wait_ge(q_stacked[c], STACK_DMAS * (b // CYC + w))
                    nc.vector.tensor_tensor(q_lo[:, c, :, :], bank[0][:, :].rearrange("p (g t) -> p g t", g=G),
                                            q_hi[:, c, :, :].bitcast(f32), ALU.subtract).then_inc(q_lo_ok, 1)

                def maxima(b, u):
                    c, blk, pair = b % CYC, u // 4, u % 4
                    dve.wait_ge(s_ps, SU * (b + o) + u + 1)
                    if u == 0 and b >= CYC:
                        dve.wait_ge(mT_ps, b + o - CYC + 1)
                    keys = 128 * (blk + 1)
                    nc.vector.tensor_reduce(neg_max[:, c, blk, 2 * pair:2 * pair + 2],
                                            bank[2 + u % 2][:, :].rearrange("p (h k) -> p h k", h=2)[:, :, 0:keys],
                                            AX.X, ALU.max, negate=True).then_inc(max_ok, 1)

                def divide(b, blk):
                    c = b % CYC
                    dve.wait_ge(pv_ps, H * TB * (b + o) + H * (blk + 1))
                    if blk == 0 and b >= CYC:
                        dve.wait_ge(yT_ps, b + o - CYC + 1)
                    y = bank[6][:, 0:H * VW].rearrange("p (h w) -> p h w", h=H)
                    nc.vector.reciprocal(rden[:, c, blk, :], y[:, :, L]).then_inc(rden_ok, 1)
                    dve.wait_ge(rden_ok, TB * (b + o) + blk + 1)
                    nc.vector.tensor_tensor(yn[:, c, blk, :, :], y[:, :, 0:L],
                                            rden[:, c, blk, :, None].to_broadcast([128, H, L]), ALU.mult).then_inc(yn_ok, 1)

                for u in range(SU):
                    if live(s - 1, looped):
                        maxima(s - 1, u)
                    if u == 4 and live(s - 3, looped):
                        divide(s - 3, 0)
                    b = s - 4
                    if u == 4 and live(b, looped):
                        c = b % CYC
                        dve.wait_ge(s_out, b + o + 1)
                        if b >= CYC:
                            dve.wait_ge(res_ok, b + o - CYC + 1)
                        nc.vector.tensor_tensor(sg[:, c, :, :], bank[7][:, 0:TB * D].rearrange("p (j d) -> p j d", j=TB),
                                                gate_all[:, bass.ds(b + o, 1), :, :].rearrange("p o j d -> p (o j) d"),
                                                ALU.mult).then_inc(sg_ok, 1)
                if live(s - 3, looped):
                    divide(s - 3, 1)
                b = s - 1
                if live(b, looped):
                    dve.wait_ge(m_hi_ok, b + o + 1)
                    if b >= 1:
                        dve.wait_ge(m_stacked, 32 * (b + o))
                    nc.vector.tensor_tensor(m_lo[:, :], bank[7][0:H, 0:T], m_hi[:, :].bitcast(f32), ALU.subtract).then_inc(m_lo_ok, 1)

            run(dve, step2, LAGS2, FIRST2)

        @block.tensor
        def _(pe):
            mm, tr = nc.tensor.matmul, nc.tensor.transpose
            pe.wait_ge(pool_const, 2)
            pe.wait_ge(ld_small, 64)
            tr(bank[7][:, 32:64], wup[:, 0, :], ident[0:L, 0:L])
            tr(bank[7][:, 64:96], wup[:, 1, :], ident[0:L, 0:L])
            tr(bank[7][:, 96:96 + E], b2_sb, ident[0:E, 0:E])
            for f in range(FB):
                last = tr(bank[7][:, 104 + E * f:104 + E * f + E], b1_sb[:, 128 * f:128 * f + 128], ident[0:E, 0:E])
            last.then_inc(small_T, 1)
            pe.wait_ge(last_step, 5)
            tr(bank[6][:, 32:32 + B], xnlast, ident[0:B, 0:B]).then_inc(last_T, 1)
            pe.wait_ge(last_cp, 1)
            mm(bank[6][:, 0:B], Wp1_sb, lastT, start=True, stop=True).then_inc(nav_ps, 1)
            pe.wait_ge(ld_wq, 16)
            for h in range(H):
                last = tr(bank[h // 4][:, 128 * (h % 4):128 * (h % 4) + 128], wq_sb[:, h, :], ident[:, :])
                if h % 4 == 3:
                    last.then_inc(wqT_ps, 1)
            pe.wait_ge(dve_const, 1)
            pe.wait_ge(nav_cp, 1)
            mm(bank[6][0:B, 64:64 + E], navT, Wp2_sb, start=True, stop=False)
            mm(bank[6][0:B, 64:64 + E], ones_row[:, 0:B], bp2_sb, start=False, stop=True).then_inc(lg_ps, 1)
            pe.wait_ge(ld_w2, 16)
            for i in range(E * FB):
                last = tr(bank[2 + i // 4][:, 128 * (i % 4):128 * (i % 4) + 128], W2_sb[:, i // FB, i % FB, :], ident[:, :])
                if i % 4 == 3:
                    last.then_inc(w2T_ps, 1)
            pe.wait_ge(sel_step, 4)
            mm(bank[6][0:1, 96:96 + B], selF, ident[0:B, 0:B], start=True, stop=True).then_inc(selT_ps, 1)
            pe.wait_ge(wqT_cp, 2)
            pe.wait_ge(tab_cp, 1)
            for h in range(H):
                last = mm(bank[0][:, L * h:L * h + L], wqT[:, h, :], wupT[:, 0, :], start=True, stop=True)
            last.then_inc(A_ps, 1)
            pe.wait_ge(ld_wo, 48)
            for h in range(H):
                r, g = h % R, h // R
                last = mm(bank[1][L * r:L * r + L, D * g:D * g + D], wupT[:, 1, :], wo_sb[:, h, :], start=True, stop=True)
            last.then_inc(U_ps, 1)
            for i in range(E * FB):
                if i % 4 == 0:
                    pe.wait_ge(w2T_cp, i // 4 + 1)
                last = mm(bank[2 + i // 4][:, 128 * (i % 4):128 * (i % 4) + 128], W2T[:, i // FB, i % FB, :], Wo_sb, start=True, stop=True)
                if i % 4 == 3:
                    last.then_inc(w2o_ps, 1)
            pe.wait_ge(sel_ready, 1)
            for e in range(E):
                at = bank[6 + e // 4][:, 128 * (e % 4):128 * (e % 4) + 128]
                mm(at, b2rep[:, e, :], Wo_sb, start=True, stop=False)
                last = mm(at, ones_row[:, :], bo_sb, start=False, stop=True)
                if e % 4 == 3:
                    last.then_inc(b2o_ps, 1)
            pe.wait_ge(A_cp, 1)
            pe.wait_ge(U_cp, 1)
            pe.wait_ge(tab_cp, 7)
            pe.wait_ge(ld_w1, 48)

            def step1(s, o, w, looped):
                b = s
                if live(b, looped):
                    c = b % CYC
                    pe.wait_ge(xn_ok, b + o + 1)
                    if b >= 1:
                        pe.wait_ge(xT_ok, b + o)
                    for j in range(TB):
                        last = tr(bank[0][:, 128 * j:128 * j + 128], xn[:, c, j, :], ident[:, :])
                    last.then_inc(xT_ps, 1)
                b = s - 3
                if live(b, looped):
                    c = b % CYC
                    pe.wait_ge(h_ok, b + o + 1)
                    if b >= CYC:
                        pe.wait_ge(z_ok, b + o - CYC + 1)
                    for j in range(TB):
                        for f in range(FB):
                            last = mm(bank[5 + c][:, D * j:D * j + D], hT[:, c, f, 128 * j:128 * j + 128],
                                      wsel[:, c, W2O_AT + D * f:W2O_AT + D * f + D], start=(f == 0), stop=(f == FB - 1))
                    last.then_inc(f2_ps, 1)
                b = s - 2
                if live(b, looped):
                    c = b % CYC
                    pe.wait_ge(xT_ok, b + o + 1)
                    if b >= 1:
                        pe.wait_ge(v_kept, b + o)
                    for j in range(TB):
                        last = mm(bank[1][:, G * L * j:G * L * (j + 1)], xT[:, c, 128 * j:128 * j + 128], wvd[:, :], start=True, stop=True)
                    last.then_inc(v_ps, 1)
                    pe.wait_ge(wsel_ok, b + o + 1)
                    if b >= CYC:
                        pe.wait_ge(h_ok, b + o - CYC + 1)
                    for f in range(FB):
                        last = mm(bank[2 + c][:, T * f:T * f + T], wsel[:, c, W1_AT + 128 * f:W1_AT + 128 * f + 128], xT[:, c, :],
                                  start=True, stop=True)
                    last.then_inc(h_ps, 1)

            run(pe, step1, LAGS1, FIRST1)
            pe.wait_ge(xT_kept, B)
            pe.wait_ge(v_kept, B)
            pe.wait_ge(h_ok, B)
            pe.wait_ge(z_ok, B)

            def step2(s, o, w, looped):
                b = s
                if live(b, looped):
                    if b >= 1:
                        pe.wait_ge(k_lo_ok, b + o)
                    xnT = xnT_all[:, bass.ds(b + o, 1), :].rearrange("p o t -> p (o t)")
                    for g in range(G):
                        last = mm(bank[1][0:KR, T * g:T * g + T], WK3[:, g, :, :].rearrange("p r l -> p (r l)"), xnT, start=True, stop=True)
                    last.then_inc(k_ps, 1)
                    if b >= 1:
                        pe.wait_ge(q_lo_ok, b + o)
                    for g in range(G):
                        last = mm(bank[0][:, T * g:T * g + T], A[:, 128 * g:128 * g + 128], xnT, start=True, stop=True)
                    last.then_inc(q_ps, 1)
                b = s - 4
                if live(b, looped):
                    c = b % CYC
                    pe.wait_ge(yn_ok, TB * (b + o + 1))
                    if live(s - 2, looped):
                        pe.wait_ge(m_lo_ok, s - 2 + o + 1)
                    for g in range(G):
                        for j in range(TB):
                            last = tr(bank[7][:, T * g + 128 * j:T * g + 128 * j + 128],
                                      yn[:, c, j, R * g:R * g + R, :].rearrange("p h l -> p (h l)"), ident[:, :])
                    last.then_inc(yT_ps, 1)

                def scores(b, u):
                    c, blk, pair = b % CYC, u // 4, u % 4
                    if u == 0:
                        pe.wait_ge(q_stacked[c], STACK_DMAS * (b // CYC + w + 1))
                        pe.wait_ge(k_lo_ok, b + o + 1)
                    if SU * b + u >= 2:
                        pe.wait_ge(max_ok, SU * (b + o) + u - 1)
                    at = bank[2 + u % 2]
                    for i in range(2):
                        h = 2 * pair + i
                        mm(at[:, T * i:T * i + T], q_stack[0:KR, c, h, 128 * blk:128 * blk + 128], k_stack[0:KR, c, h // R, :],
                           start=(i == 0), stop=False)
                    mm(at[:, :].rearrange("p (h k) -> p h k", h=2)[:, :, 128 * blk:128 * blk + 128], identb[:, :], causal[:, :, :],
                       start=False, stop=True).then_inc(s_ps, 1)

                def shifted(b, t):
                    c, g, part = b % CYC, t // 3, t % 3
                    if t == 0:
                        pe.wait_ge(m_stacked, 32 * (b + o + 1))
                    if PU * b + t >= 2:
                        pe.wait_ge(exp_ok, PU * (b + o) + t - 1)
                    kb = part // 2
                    if kb == 0:
                        q = q_stack[0:KM, c, R * g + 2 * part:R * g + 2 * part + 2, :]
                    else:
                        q = q_stack[0:KM, c, R * g:R * g + R, 128:256]
                    mm(bank[4 + t % 2][:, :], k_stack[0:KM, c, g, 128 * kb:128 * kb + 128], q, start=True, stop=True).then_inc(st_ps, 1)

                def weighted(b, blk, h):
                    c, g, r = b % CYC, h // R, h % R
                    if blk == 0 and h == 0:
                        pe.wait_ge(vw_ok, b + o + 1)
                        pe.wait_ge(causal_ok, PU * (b + o + 1))
                        if b >= 1:
                            pe.wait_ge(yn_ok, TB * (b + o))
                    if blk == 1 and h == 0:
                        pe.wait_ge(yn_ok, TB * (b + o) + 1)
                    at = bank[6][:, VW * h:VW * h + VW]
                    n = PU * b + 3 * g
                    first = probs[:, (n + r // 2) % RING, T * (r % 2) + 128 * blk:T * (r % 2) + 128 * blk + 128]
                    last = mm(at, first, v_w[:, c, 0, g, :], start=True, stop=(blk == 0))
                    if blk == 1:
                        second = probs[:, (n + 2) % RING, 128 * r:128 * r + 128]
                        last = mm(at, second, v_w[:, c, 1, g, :], start=False, stop=True)
                    last.then_inc(pv_ps, 1)

                for u in range(SU):
                    if live(s - 1, looped):
                        scores(s - 1, u)
                    if u >= 2 and live(s - 2, looped):
                        shifted(s - 2, u - 2)
                    if live(s - 3, looped):
                        for h in (2 * (u % 4), 2 * (u % 4) + 1):
                            weighted(s - 3, u // 4, h)
                    b = s - 4
                    if u == 3 and live(b, looped):
                        pe.wait_ge(yT_ok, b + o + 1)
                        for j in range(TB):
                            for g in range(G):
                                last = mm(bank[7][:, D * j:D * j + D], yT[:, g, 128 * j:128 * j + 128], U[:, g, :], start=(g == 0), stop=(g == G - 1))
                        last.then_inc(s_out, 1)
                b = s - 1
                if live(b, looped):
                    c = b % CYC
                    pe.wait_ge(max_ok, SU * (b + o + 1))
                    if live(s - 4, looped):
                        pe.wait_ge(sg_ok, s - 4 + o + 1)
                    for j in range(TB):
                        last = tr(bank[7][0:H, 128 * j:128 * j + 128], neg_max[:, c, j, :], ident[:, :])
                    last.then_inc(mT_ps, 1)

            run(pe, step2, LAGS2, FIRST2)


_INS = ["L0_attn_x", "L0_attn_wq", "L0_attn_wk_down", "L0_attn_wv_down", "L0_attn_wk_up", "L0_attn_wv_up", "L0_attn_wo",
        "L0_ffn_Wp1", "L0_ffn_bp1", "L0_ffn_Wp2", "L0_ffn_bp2", "L0_ffn_W1", "L0_ffn_b1", "L0_ffn_W2", "L0_ffn_b2",
        "L0_ffn_Wo", "L0_ffn_bo"]


def kernel(**inputs):
    import concourse.bacc as bacc
    from concourse.bass_utils import run_bass_kernel_spmd

    nc = bacc.Bacc("TRN2", target_bir_lowering=False, num_devices=1)
    arrays, args = {}, []
    for name in _INS:
        a = np.ascontiguousarray(inputs[name])
        arrays[name] = a
        args.append(nc.dram_tensor(name, a.shape, mybir.dt.from_np(a.dtype), kind="ExternalInput").ap())
    shape = arrays["L0_attn_x"].shape
    args.append(nc.dram_tensor("out", shape, mybir.dt.float32, kind="ExternalOutput").ap())
    layernorm_mla_attention_times_routed_ffn_gate(nc, *args)
    return run_bass_kernel_spmd(nc, [arrays], core_ids=[0]).results[0]["out"]
```

```python
import concourse.bass as bass
from concourse import mybir
from contextlib import ExitStack
import numpy as np


def layernorm_mla_attention_times_routed_ffn_gate(
    nc, x, wq, wk_down, wv_down, wk_up, wv_up, wo,
    Wp1, bp1, Wp2, bp2, W1, b1, W2, b2, Wo, bo, out,
):
    f32, f32r, bf16, f16 = mybir.dt.float32, mybir.dt.float32r, mybir.dt.bfloat16, mybir.dt.float16
    i32, u32 = mybir.dt.int32, mybir.dt.uint32
    ALU, ACT, AX = mybir.AluOpType, mybir.ActivationFunctionType, mybir.AxisListType

    B, T, D = x.shape
    L = wk_up.shape[0]
    G = wk_down.shape[1] // L
    HD = wk_up.shape[1]
    H = wq.shape[1] // HD
    R = H // G
    E, _, F = W1.shape
    FB, TB = F // 128, T // 128
    VW = L + 1
    VP = 2 * L + 2
    SCALE = float(HD) ** -0.5
    MASKED = -1e30
    EPS = 1e-5
    W1_AT, W2O_AT, B2O_AT, B1_AT = 0, F, 2 * F, 2 * F + D
    EW = B1_AT + FB
    KR = 3 * L
    KM = KR + 1
    SU = 8
    PU = 6
    CYC = 4

    ctx = ExitStack()
    with ctx:
        def sb(name, shape, dt=f32):
            return ctx.enter_context(nc.sbuf_tensor(name, shape, dt))

        def sem(name):
            return ctx.enter_context(nc.semaphore(name))

        xnT_all = sb("xnT_all", [128, B, T])
        gate_all = sb("gate_all", [128, B, TB, D])
        v_all = sb("v_all", [128, B, TB, G, VP], f16)
        A = sb("A", [128, H * L])
        WK3 = sb("WK3", [128, G, 3, L])
        wvd = sb("wvd", [128, G * L])
        U = sb("U", [128, G, D])
        ident = sb("ident", [128, 128])
        identb = sb("identb", [128, 128], bf16)
        causal = sb("causal", [128, 2, 128], bf16)
        ones_row = sb("ones_row", [1, 128])
        neg_half = sb("neg_half", [128, TB])
        sel_row = sb("sel_row", [1, B], i32)
        BIG = (2 + 1) * PU * 512
        big = sb("big", [128, BIG])
        table = big[:, 0:E * EW].rearrange("p (e w) -> p e w", e=E)
        o = E * EW
        wsel = big[:, o:o + CYC * EW].rearrange("p (c w) -> p c w", c=CYC)
        o += CYC * EW
        hT = big[:, o:o + 2 * FB * T].rearrange("p (c f t) -> p c f t", c=2, f=FB)
        o += 2 * FB * T
        assert o <= BIG
        parts = big[:, 0:2 * PU * 512].bitcast(f16).rearrange("p (i c u n) -> p i c u n", i=2, c=2, u=PU)
        p_hi, p_lo = parts[:, 0, :, :, :], parts[:, 1, :, :, :]
        probs = big[:, 2 * PU * 512:BIG].rearrange("p (u n) -> p u n", u=PU)
        flat = gate_all[:, :, :, :].rearrange("p b j d -> p (b j d)")
        W2T = flat[:, 0:2048].rearrange("p (e f j) -> p e f j", e=E, f=FB)
        wqT = flat[:, 2048:3072].rearrange("p (h d) -> p h d", h=H)
        b2rep = flat[:, 3072:4096].rearrange("p (e j) -> p e j", e=E)
        flat2 = xnT_all[:, :, :].rearrange("p b t -> p (b t)")
        W2_sb = flat2[:, 0:2048].rearrange("p (e f h) -> p e f h", e=E, f=FB)
        wq_sb = flat2[:, 2048:3072].rearrange("p (h d) -> p h d", h=H)
        wo_sb = flat2[:, 3072:4096].rearrange("p (h d) -> p h d", h=H)
        Wo_sb = flat2[:, 4096:4224]
        wup = flat2[0:L, 4224:4480].rearrange("l (k d) -> l k d", k=2)
        b1_sb = flat2[0:E, 4480:4736]
        b2_sb = flat2[0:E, 4736:4864]
        bo_sb = flat2[0:1, 4864:4992]
        Wp1_sb = flat2[:, 4992:5120]
        Wp2_sb = flat2[:, 5120:5128]
        bp1_sb = flat2[:, 5128:5129]
        bp2_sb = flat2[0:1, 5136:5144]
        wkd_sb = flat2[:, 5144:5208].rearrange("p (g l) -> p g l", g=G)
        xlast = flat2[0:B, 5248:5376]
        xnlast = flat2[0:B, 5376:5504]
        lastT = flat2[:, 5504:5504 + B]
        navT = flat2[:, 5536:5536 + B]
        logits = flat2[0:B, 5568:5576]
        top8 = flat2[0:B, 5576:5584]
        wupT = flat2[:, 5600:5664].rearrange("p (k l) -> p k l", k=2)
        st_last = flat2[0:B, 5664:5670]
        mv_last = flat2[0:B, 5672:5674]
        rs_last = flat2[0:B, 5674:5675]
        selF = flat2[0:B, 5675:5676]
        wvd_in = flat2[:, 5680:5744].rearrange("p (g l) -> p g l", g=G)
        wvd_rep = flat2[:, 5744:6000].rearrange("p (g r l) -> p g r l", g=G, r=R)
        wvdT = flat2[0:L, 6000:6256].rearrange("l (g d) -> l g d", g=G)
        col_max = flat2[:, 6256:6256 + G]
        col_rcp = flat2[:, 6258:6258 + G]
        sel_idx = sb("sel_idx", [B, 8], u32)
        x_in = sb("x_in", [128, CYC, TB, D])
        xn = sb("xn", [128, CYC, TB, D])
        xT = sb("xT", [128, 2, T])
        stats = sb("stats", [128, 2, TB, 6])
        mv = sb("mv", [128, CYC, TB, 2])
        var_eps = sb("var_eps", [128, 2, TB])
        rstd = sb("rstd", [128, CYC, TB])
        xb = sb("xb", [128, 2, TB, D])
        z = sb("z", [128, 2, TB, D])
        th = sb("th", [128, 2, TB, D])
        q_hi = sb("q_hi", [128, 2, G, T], f32r)
        q_lo = sb("q_lo", [128, 2, G, T], f32r)
        q_stack = sb("q_stack", [128, CYC, H, T], f32r)
        k_stack = sb("k_stack", [128, CYC, G, T], f32r)
        neg_max = sb("neg_max", [128, 2, TB, H])
        m_row = sb("m_row", [H, T], f32r)
        v_w = sb("v_w", [128, 2, TB, G, VP], f16)
        rden = sb("rden", [128, 2, TB, H])
        yn = xn[:, :, :, :].rearrange("p (c e) j d -> p c (e j d)", c=2).rearrange("p c (j h l) -> p c j h l", j=TB, h=H)
        yT = xT
        sg, res = xb, z

        bank = [ctx.enter_context(nc.psum_tensor(f"bank{i}", [128, 512], f32)) for i in range(8)]

        ld_router, ld_small, ld_wq, ld_w2 = sem("ld_router"), sem("ld_small"), sem("ld_wq"), sem("ld_w2")
        ld_wo, ld_w1 = sem("ld_wo"), sem("ld_w1")
        pool_set, pool_const = sem("pool_set"), sem("pool_const")
        dve_const = sem("dve_const")
        wk3_ready = sem("wk3_ready")
        last_step = sem("last_step")
        small_T, small_cp = sem("small_T"), sem("small_cp")
        last_T, last_cp = sem("last_T"), sem("last_cp")
        nav_ps, nav_cp = sem("nav_ps"), sem("nav_cp")
        lg_ps, sel_step = sem("lg_ps"), sem("sel_step")
        selT_ps, sel_ready = sem("selT_ps"), sem("sel_ready")
        wqT_ps, wqT_cp = sem("wqT_ps"), sem("wqT_cp")
        w2T_ps, w2T_cp = sem("w2T_ps"), sem("w2T_cp")
        A_ps, U_ps, w2o_ps, b2o_ps = sem("A_ps"), sem("U_ps"), sem("w2o_ps"), sem("b2o_ps")
        A_cp, U_cp, tab_cp = sem("A_cp"), sem("U_cp"), sem("tab_cp")
        rep_ok, wvT_ps, wv_step, wvd_ps, wvd_ok = sem("rep_ok"), sem("wvT_ps"), sem("wv_step"), sem("wvd_ps"), sem("wvd_ok")
        bn_st, bn_ag = sem("bn_st"), sem("bn_ag")
        x1_ld = [sem(f"x1_ld{c}") for c in range(CYC)]
        eps_add, rstd_ok, xn_ok = sem("eps_add"), sem("rstd_ok"), sem("xn_ok")
        xT_ps, xT_ok, xT_kept, xb_ok = sem("xT_ps"), sem("xT_ok"), sem("xT_kept"), sem("xb_ok")
        wsel_ld = [sem(f"wsel_ld{c}") for c in range(CYC)]
        v_ps, v_hi_ok, v_kept, h_ps, h_ok, f2_ps, z_ok = (sem(n) for n in (
            "v_ps", "v_hi_ok", "v_kept", "h_ps", "h_ok", "f2_ps", "z_ok"))
        th_ok, gate_ok = sem("th_ok"), sem("gate_ok")
        k_ps, q_ps, k_hi_ok, q_hi_ok, k_lo_ok, q_lo_ok = (sem(n) for n in (
            "k_ps", "q_ps", "k_hi_ok", "q_hi_ok", "k_lo_ok", "q_lo_ok"))
        m_stacked = [sem(f"m_stacked{c}") for c in range(2)]
        q_stacked = [sem(f"q_stacked{c}") for c in range(CYC)]
        s_ps, max_ok, mT_ps, m_row_ok = (sem(n) for n in ("s_ps", "max_ok", "mT_ps", "m_row_ok"))
        st_ps, exp_ok, causal_ok = sem("st_ps"), sem("exp_ok"), sem("causal_ok")
        p_hi_ok, lo_dve, lo_pool = sem("p_hi_ok"), sem("lo_dve"), sem("lo_pool")
        vw_ld = [sem(f"vw_ld{c}") for c in range(2)]
        pv_ps, rden_ok, yn_ok = sem("pv_ps"), sem("rden_ok"), sem("yn_ok")
        yT_ps, yT_ok, s_out, sg_ok, res_ok = (sem(n) for n in ("yT_ps", "yT_ok", "s_out", "sg_ok", "res_ok"))
        x2_ld = [sem(f"x2_ld{c}") for c in range(CYC)]
        out_st = [sem(f"out_st{c}") for c in range(2)]

        block = ctx.enter_context(nc.Block())

        STACK_DMAS = 3 * R * 16
        x_v = x.rearrange("b (j p) d -> b p j d", p=128)
        out_v = out.rearrange("b (j p) d -> b p j d", p=128)

        def run(eng, step, lags, first, lead=0):
            turns = (B - lead - first) // CYC
            for s in range(first):
                step(s, 0, 0, False)
            with eng.Fori(0, turns) as i:
                for s in range(first, first + CYC):
                    step(s, i * CYC, i, True)
            for s in range(first + turns * CYC, B + lags):
                step(s, 0, 0, False)

        LAGS1, FIRST1 = 6, 10
        LAGS2, FIRST2 = 6, 10

        def uses(b, w, n):
            return b // n + (CYC // n) * w

        def count(eng, n, looped):
            return eng.snap(eng.to_reg(n)) if looped else n

        def live(b, looped):
            return looped or 0 <= b < B

        @block.sync
        def _(sp):
            ld = sp.dma_start
            ld(xlast, x[:, T - 1, :]).then_inc(ld_router, 16)
            ld(Wp1_sb, Wp1).then_inc(ld_router, 16)
            ld(bp1_sb, bp1.rearrange("(n o) -> n o", o=1)).then_inc(ld_router, 16)
            ld(Wp2_sb, Wp2).then_inc(ld_router, 16)
            ld(bp2_sb, bp2.rearrange("(o n) -> o n", o=1)).then_inc(ld_router, 16)
            ld(wup[:, 0, :], wk_up).then_inc(ld_small, 16)
            ld(wup[:, 1, :], wv_up).then_inc(ld_small, 16)
            ld(b1_sb, b1).then_inc(ld_small, 16)
            ld(b2_sb, b2).then_inc(ld_small, 16)
            ld(wq_sb, wq.rearrange("p (h d) -> p h d", h=H)).then_inc(ld_wq, 16)
            ld(W2_sb, W2.rearrange("e (f p) h -> p e f h", p=128)).then_inc(ld_w2, 16)
            ld(Wo_sb, Wo).then_inc(ld_wo, 16)
            ld(bo_sb, bo.rearrange("(o n) -> o n", o=1)).then_inc(ld_wo, 16)
            ld(wo_sb, wo.rearrange("(h p) o -> p h o", p=128)).then_inc(ld_wo, 16)
            ld(table[:, :, W1_AT:W1_AT + F], W1.rearrange("e p f -> p e f")).then_inc(ld_w1, 16)
            ld(wkd_sb, wk_down.rearrange("p (g l) -> p g l", g=G)).then_inc(ld_w1, 16)
            ld(wvd_in, wv_down.rearrange("p (g l) -> p g l", g=G)).then_inc(ld_w1, 16)

            def load_x(b, o, done, c):
                sp.dma_start(x_in[:, c, :, :], x_v[bass.ds(b + o, 1), :, :, :].rearrange("o p j d -> p (o j) d")).then_inc(done[c], 16)

            for b in range(2):
                load_x(b, 0, x1_ld, b)

            def step1(s, o, w, looped):
                b = s + 2
                if live(b, looped):
                    c = b % CYC
                    sp.wait_ge(ld_router, 80)
                    if b >= CYC:
                        sp.wait_ge(xn_ok, b + o - CYC + 1)
                    load_x(b, o, x1_ld, c)
                b = s - 1
                if live(b, looped):
                    c = b % CYC
                    if b == 0:
                        for q in (tab_cp, 7), (ld_w1, 48), (sel_ready, 1):
                            sp.wait_ge(*q)
                    expert = sp.value_load(sel_row[0:1, bass.ds(b + o, 1)], min_val=0, max_val=E - 1)
                    sp.wait_ge(ld_router, 80)
                    if b >= CYC:
                        sp.wait_ge(f2_ps, b + o - CYC + 1)
                        sp.wait_ge(h_ok, b + o - CYC + 1)
                        sp.wait_ge(xb_ok, b + o - CYC + 1)
                    sp.dma_start(wsel[:, c, :], table[:, bass.ds(expert, 1), :].rearrange("p o w -> p (o w)")).then_inc(wsel_ld[c], 16)

            run(sp, step1, LAGS1, FIRST1, lead=2)

            def step2(s, o, w, looped):
                b = s - 3
                if live(b, looped):
                    sp.wait_ge(m_row_ok, b + o + 1)
                    sp.dma_start(q_stack[KR:KM, b % CYC, :, :].bitcast(f32), m_row[:, :].bitcast(f32)).then_inc(m_stacked[b % 2], 16)
                b = s - 3
                if live(b, looped):
                    sp.wait_ge(ld_router, 80)
                    if b == 0:
                        sp.wait_ge(v_kept, B)
                    if b >= 2:
                        sp.wait_ge(pv_ps, H * TB * (b + o - 1))
                    sp.dma_start(v_w[:, b % 2, :, :, :].rearrange("p j g w -> p (j g w)"),
                                 v_all[:, bass.ds(b + o, 1), :, :, :].rearrange("p o j g w -> p (o j g w)")).then_inc(vw_ld[b % 2], 16)
                b = s - 5
                if live(b, looped):
                    c = b % CYC
                    sp.wait_ge(ld_router, 80)
                    if b >= CYC:
                        sp.wait_ge(res_ok, b + o - CYC + 1)
                    elif b == 0:
                        sp.wait_ge(xn_ok, B)
                    load_x(b, o, x2_ld, c)
                b = s
                if live(b, looped):
                    c = b % CYC
                    made = count(sp, b + o + 1, looped)
                    if b >= CYC:
                        sp.wait_ge(st_ps, PU * (b + o - CYC + 1))
                    for part, at in ((q_hi, 0), (q_hi, 2), (q_lo, 1)):
                        if at == 0:
                            sp.wait_ge(q_hi_ok, made)
                        if at == 1:
                            sp.wait_ge(q_lo_ok, made)
                        for r in range(R):
                            sp.dma_start(q_stack[at * L:at * L + L, c, r:H:R, :].bitcast(f32),
                                         part[r * L:r * L + L, b % 2, :, :].bitcast(f32)).then_inc(q_stacked[c], 16)
                b = s - 6
                if live(b, looped):
                    sp.wait_ge(ld_router, 80)
                    sp.wait_ge(res_ok, b + o + 1)
                    sp.dma_start(out_v[bass.ds(b + o, 1), :, :, :].rearrange("o p j d -> p (o j) d"), res[:, b % 2, :, :]).then_inc(out_st[b % 2], 16)

            run(sp, step2, LAGS2, FIRST2)
            for c in range(2):
                sp.wait_ge(out_st[c], 16 * (B // 2))

        @block.gpsimd
        def _(pool):
            nc.gpsimd.memset(ident[:, :], 0.0).then_inc(pool_set, 1)
            nc.gpsimd.memset(causal[:, :, :], 0.0).then_inc(pool_set, 1)
            nc.gpsimd.memset(neg_half[:, :], -0.5)
            pool.wait_ge(pool_set, 1)
            nc.gpsimd.affine_select(out=ident[:, :], in_=ident[:, :], compare_op=ALU.not_equal, fill=1.0,
                                    base=0, pattern=[[-1, 128]], channel_multiplier=1).then_inc(pool_const, 1)
            pool.wait_ge(pool_set, 2)
            nc.gpsimd.affine_select(out=causal[:, :, :], in_=causal[:, :, :], compare_op=ALU.is_ge, fill=MASKED,
                                    base=0, pattern=[[0, 2], [-1, 128]], channel_multiplier=1)
            pool.wait_ge(pool_const, 1)
            nc.gpsimd.tensor_copy(identb[:, :], ident[:, :]).then_inc(pool_const, 1)
            pool.wait_ge(last_step, 2)
            nc.gpsimd.tensor_scalar(rs_last, mv_last[:, 1:2], EPS, None, ALU.add).then_inc(last_step, 1)
            pool.wait_ge(last_step, 3)
            nc.gpsimd.tensor_tensor(rs_last, rs_last, neg_half[0:B, 0:1], ALU.pow).then_inc(last_step, 1)
            pool.wait_ge(ld_w1, 48)
            for r in range(3):
                last = nc.gpsimd.tensor_copy(WK3[:, :, r, :], wkd_sb)
            last.then_inc(wk3_ready, 1)
            for r in range(R):
                last = nc.gpsimd.tensor_copy(wvd_rep[:, :, r, :], wvd_in)
            last.then_inc(rep_ok, 1)

            def step1(s, o, w, looped):
                b = s
                if live(b, looped):
                    c = b % CYC
                    made = count(pool, b + o + 1, looped)
                    pool.wait_ge(pool_const, 2)
                    pool.wait_ge(bn_ag, made)
                    nc.gpsimd.tensor_scalar(var_eps[:, b % 2, :], mv[:, c, :, 1], EPS, None, ALU.add).then_inc(eps_add, 1)
                    pool.wait_ge(eps_add, b + o + 1)
                    if b >= CYC:
                        pool.wait_ge(xn_ok, b + o - CYC + 1)
                    nc.gpsimd.tensor_tensor(rstd[:, c, :], var_eps[:, b % 2, :], neg_half[:, :], ALU.pow).then_inc(rstd_ok, 1)
                b = s - 4
                if live(b, looped):
                    c = b % CYC
                    pool.wait_ge(xn_ok, b + o + 1)
                    pool.wait_ge(wsel_ld[c], 16 * (uses(b, w, CYC) + 1))
                    if b >= 2:
                        pool.wait_ge(z_ok, b + o - 1)
                    for j in range(TB):
                        last = nc.gpsimd.tensor_tensor(xb[:, b % 2, j, :], xn[:, c, j, :], wsel[:, c, B2O_AT:B2O_AT + D], ALU.add)
                    last.then_inc(xb_ok, 1)

            run(pool, step1, LAGS1, FIRST1)

            def step2(s, o, w, looped):
                def cut(b, t):
                    made = count(pool, PU * (b + o) + t + 1, looped)
                    pool.wait_ge(pool_const, 2)
                    pool.wait_ge(exp_ok, made)
                    if t % 3 < 2:
                        upper = probs[:, t, :].rearrange("p (h q) -> p h q", h=2)[:, :, 0:128]
                        heads = 2
                    else:
                        upper = probs[:, t, :].rearrange("p (h q) -> p h q", h=R)
                        heads = R
                    nc.gpsimd.affine_select(out=upper, in_=upper, compare_op=ALU.is_ge, fill=0.0, base=0,
                                            pattern=[[0, heads], [1, 128]], channel_multiplier=-1).then_inc(causal_ok, 1)

                def remainder(b, t):
                    pool.wait_ge(p_hi_ok, PU * (b + o) + t + 1)
                    if b >= 2:
                        pool.wait_ge(pv_ps, H * TB * (b + o - 1))
                    nc.gpsimd.tensor_tensor(p_lo[:, b % 2, t, :], probs[:, t, :], p_hi[:, b % 2, t, :], ALU.subtract).then_inc(lo_pool, 1)

                if live(s - 4, looped):
                    remainder(s - 4, 2)
                    cut(s - 4, PU - 1)
                b = s - 6
                if live(b, looped):
                    pool.wait_ge(sg_ok, b + o + 1)
                    pool.wait_ge(x2_ld[b % CYC], 16 * (uses(b, w, CYC) + 1))
                    if b >= 2:
                        pool.wait_ge(out_st[b % 2], 16 * uses(b, w, 2))
                    nc.gpsimd.tensor_tensor(res[:, b % 2, :, :], sg[:, b % 2, :, :], x_in[:, b % CYC, :, :], ALU.add).then_inc(res_ok, 1)
                if live(s - 4, looped):
                    remainder(s - 4, PU - 1)
                if live(s - 3, looped):
                    for t in range(PU - 1):
                        cut(s - 3, t)

            run(pool, step2, LAGS2, FIRST2)

        @block.scalar
        def _(act):
            act.wait_ge(nav_ps, 1)
            nc.scalar.activation(navT, bank[6][:, 0:B], ACT.Gelu, bias=bp1_sb).then_inc(nav_cp, 1)
            for i in range(4):
                act.wait_ge(w2T_ps, i + 1)
                nc.scalar.copy(flat[:, 512 * i:512 * i + 512], bank[2 + i][:, :]).then_inc(w2T_cp, 1)
            act.wait_ge(A_ps, 1)
            nc.scalar.mul(A[:, :], bank[0][:, 0:H * L], SCALE).then_inc(A_cp, 1)
            for i in range(4):
                act.wait_ge(w2o_ps, i + 1)
                nc.scalar.mul(table[:, 2 * i:2 * i + 2, W2O_AT:W2O_AT + F],
                              bank[2 + i][:, :].rearrange("p (e n) -> p e n", e=2), 0.3).then_inc(tab_cp, 1)

            def step1(s, o, w, looped):
                b = s - 5
                if live(b, looped):
                    act.wait_ge(z_ok, b + o + 1)
                    if b >= 2:
                        act.wait_ge(gate_ok, b + o - 1)
                    nc.scalar.activation(th[:, b % 2, :, :], z[:, b % 2, :, :], ACT.Tanh, scale=0.5).then_inc(th_ok, 1)
                b = s - 3
                if live(b, looped):
                    if b == 0:
                        for q in (tab_cp, 7), (A_cp, 1), (U_cp, 1), (wk3_ready, 1), (wvd_ok, 1), (selT_ps, 1):
                            act.wait_ge(*q)
                    act.wait_ge(xT_ok, b + o + 1)
                    nc.scalar.copy(xnT_all[:, bass.ds(b + o, 1), :].rearrange("p o t -> p (o t)"), xT[:, b % 2, :]).then_inc(xT_kept, 1)
                    act.wait_ge(v_ps, b + o + 1)
                    nc.scalar.copy(v_all[:, bass.ds(b + o, 1), :, :, 0:L].rearrange("p o j g l -> p (o j) g l"),
                                   bank[(1, 7)[b % 2]][:, 0:TB * G * L].rearrange("p (j g l) -> p j g l", j=TB, g=G)).then_inc(v_hi_ok, 1)
                    if b >= 2:
                        act.wait_ge(f2_ps, b + o - 1)
                    act.wait_ge(wsel_ld[b % CYC], 16 * (uses(b, w, CYC) + 1))
                    act.wait_ge(h_ps, b + o + 1)
                    for f in range(FB):
                        last = nc.scalar.activation(hT[:, b % 2, f, :], bank[2 + b % 2][:, f * T:f * T + T], ACT.Gelu,
                                                    bias=wsel[:, b % CYC, B1_AT + f:B1_AT + f + 1])
                    last.then_inc(h_ok, 1)

            run(act, step1, LAGS1, FIRST1)

            def step2(s, o, w, looped):
                def exponent(b, t):
                    if b == 0 and t == 0:
                        act.wait_ge(gate_ok, B)
                    if b >= 1:
                        if t % 3 < 2:
                            act.wait_ge(lo_dve, 4 * (b + o - 1) + 2 * (t // 3) + t % 3 + 1)
                        else:
                            act.wait_ge(lo_pool, 2 * (b + o - 1) + t // 3 + 1)
                    act.wait_ge(st_ps, PU * (b + o) + t + 1)
                    nc.scalar.activation(probs[:, t, :], bank[4 + t % 2][:, :], ACT.Exp).then_inc(exp_ok, 1)

                def leading(b, t):
                    if b >= 2:
                        act.wait_ge(pv_ps, H * TB * (b + o - 1))
                    act.wait_ge(causal_ok, PU * (b + o) + t + 1)
                    nc.scalar.copy(p_hi[:, b % 2, t, :], probs[:, t, :]).then_inc(p_hi_ok, 1)

                b = s - 3
                if live(b, looped):
                    act.wait_ge(mT_ps, b + o + 1)
                    if b >= 1:
                        act.wait_ge(m_stacked[(b - 1) % 2], 16 * (uses(b - 1, w, 2) + 1))
                    nc.scalar.copy(m_row[:, :], bank[0][0:H, 0:T]).then_inc(m_row_ok, 1)
                if live(s - 4, looped):
                    exponent(s - 4, PU - 1)
                    leading(s - 4, 3)
                b = s
                if live(b, looped):
                    if b >= 2:
                        act.wait_ge(q_stacked[(b - 2) % CYC], STACK_DMAS * (uses(b - 2, w, CYC) + 1))
                        act.wait_ge(q_lo_ok, b + o - 1)
                    act.wait_ge(q_ps, b + o + 1)
                    nc.scalar.copy(q_hi[:, b % 2, :, :], bank[0][:, :].rearrange("p (g t) -> p g t", g=G)).then_inc(q_hi_ok, 1)
                if live(s - 4, looped):
                    leading(s - 4, 4)
                    leading(s - 4, 5)
                if live(s - 3, looped):
                    exponent(s - 3, 0)
                    exponent(s - 3, 1)
                b = s - 5
                if live(b, looped):
                    act.wait_ge(yT_ps, b + o + 1)
                    if b >= 1:
                        act.wait_ge(s_out, b + o)
                    nc.scalar.copy(yT[:, :, :], bank[7][:, :].rearrange("p (g t) -> p g t", g=G)).then_inc(yT_ok, 1)
                if live(s - 3, looped):
                    leading(s - 3, 0)
                    exponent(s - 3, 2)
                b = s
                if live(b, looped):
                    c = b % CYC
                    if b >= CYC:
                        act.wait_ge(st_ps, PU * (b + o - CYC + 1))
                    act.wait_ge(k_ps, b + o + 1)
                    nc.scalar.copy(k_stack[0:KR, c, :, :], bank[0][0:KR, :].rearrange("p (g t) -> p g t", g=G)).then_inc(k_hi_ok, 1)
                if live(s - 3, looped):
                    leading(s - 3, 1)
                    exponent(s - 3, 3)
                    leading(s - 3, 2)
                    exponent(s - 3, 4)

            run(act, step2, LAGS2, FIRST2)

        @block.vector
        def _(dve):
            nc.vector.memset(ones_row[:, :], 1.0)
            nc.vector.memset(v_all[:, :, :, :, L:VW], 1.0)
            nc.vector.memset(v_all[:, :, :, :, VP - 1:VP], 0.0)
            nc.vector.memset(k_stack[KR:KM, :, :, :].bitcast(f32), 1.0).then_inc(dve_const, 1)
            dve.wait_ge(ld_router, 80)
            nc.vector.bn_stats(st_last, xlast).then_inc(last_step, 1)
            dve.wait_ge(last_step, 1)
            nc.vector.bn_aggr(mv_last, st_last).then_inc(last_step, 1)
            dve.wait_ge(last_step, 4)
            nc.vector.tensor_scalar(xnlast, xlast, mv_last[:, 0:1], rs_last, ALU.subtract, ALU.mult).then_inc(last_step, 1)
            dve.wait_ge(last_T, 1)
            nc.vector.tensor_copy(lastT, bank[6][:, 32:32 + B]).then_inc(last_cp, 1)
            dve.wait_ge(small_T, 1)
            nc.vector.tensor_copy(wupT, bank[7][:, 32:96].rearrange("p (k l) -> p k l", k=2))
            nc.vector.tensor_copy(b2rep, bank[7][:, 96:96 + E, None].to_broadcast([128, E, 128]))
            nc.vector.tensor_copy(table[:, :, B1_AT:B1_AT + FB],
                                  bank[7][:, 104:104 + E * FB].rearrange("p (f e) -> p e f", f=FB)).then_inc(tab_cp, 1)
            for i in range(2):
                dve.wait_ge(wqT_ps, i + 1)
                nc.vector.tensor_copy(wqT[:, 4 * i:4 * i + 4, :], bank[i][:, :].rearrange("p (h d) -> p h d", h=4)).then_inc(wqT_cp, 1)
            dve.wait_ge(lg_ps, 1)
            nc.vector.tensor_copy(logits, bank[6][0:B, 64:64 + E]).then_inc(sel_step, 1)
            dve.wait_ge(sel_step, 1)
            nc.vector.max(top8, logits).then_inc(sel_step, 1)
            dve.wait_ge(sel_step, 2)
            nc.vector.max_index(sel_idx[:, :], top8, logits).then_inc(sel_step, 1)
            dve.wait_ge(sel_step, 3)
            nc.vector.tensor_copy(selF, sel_idx[:, 0:1]).then_inc(sel_step, 1)
            dve.wait_ge(selT_ps, 1)
            nc.vector.tensor_copy(sel_row[:, :], bank[6][0:1, 96:96 + B]).then_inc(sel_ready, 1)
            dve.wait_ge(wvT_ps, 1)
            wvT = bank[7][:, 0:G * 128].rearrange("p (g d) -> p g d", g=G)
            nc.vector.tensor_reduce(col_max, wvT, AX.X, ALU.max, apply_absolute_value=True).then_inc(wv_step, 1)
            dve.wait_ge(wv_step, 1)
            nc.vector.tensor_scalar(col_max, col_max, 1e-30, None, ALU.max).then_inc(wv_step, 1)
            dve.wait_ge(wv_step, 2)
            nc.vector.reciprocal(col_rcp, col_max).then_inc(wv_step, 1)
            dve.wait_ge(wv_step, 3)
            for g in range(G):
                last = nc.vector.tensor_scalar(wvdT[:, g, :], wvT[0:L, g, :], col_rcp[0:L, g:g + 1], None, ALU.mult)
            last.then_inc(wv_step, 1)
            dve.wait_ge(wvd_ps, 1)
            nc.vector.tensor_copy(wvd[:, :], bank[7][:, 256:256 + G * L]).then_inc(wvd_ok, 1)
            dve.wait_ge(U_ps, 1)
            for g in range(G):
                last = nc.vector.tensor_scalar(U[:, g, :], bank[1][:, D * g:D * g + D], col_max[:, g:g + 1], 0.5, ALU.mult, ALU.mult)
            last.then_inc(U_cp, 1)
            for i in range(2):
                dve.wait_ge(b2o_ps, i + 1)
                nc.vector.tensor_scalar(table[:, 4 * i:4 * i + 4, B2O_AT:B2O_AT + D],
                                        bank[6 + i][:, :].rearrange("p (e o) -> p e o", e=4), 0.3, None, ALU.mult).then_inc(tab_cp, 1)

            def step1(s, o, w, looped):
                b = s - 1
                if live(b, looped):
                    c = b % CYC
                    dve.wait_ge(rstd_ok, b + o + 1)
                    if b >= CYC:
                        dve.wait_ge(xb_ok, b + o - CYC + 1)
                        dve.wait_ge(xT_ps, b + o - CYC + 1)
                    for j in range(TB):
                        last = nc.vector.tensor_scalar(xn[:, c, j, :], x_in[:, c, j, :], mv[:, c, j, 0:1], rstd[:, c, j:j + 1],
                                                       ALU.subtract, ALU.mult)
                    last.then_inc(xn_ok, 1)
                b = s - 6
                if live(b, looped):
                    dve.wait_ge(th_ok, b + o + 1)
                    nc.vector.scalar_tensor_tensor(out=gate_all[:, bass.ds(b + o, 1), :, :].rearrange("p o j d -> p (o j d)"),
                                                   in0=th[:, b % 2, :, :].rearrange("p j d -> p (j d)"), scalar=1.0,
                                                   in1=z[:, b % 2, :, :].rearrange("p j d -> p (j d)"),
                                                   op0=ALU.add, op1=ALU.mult).then_inc(gate_ok, 1)
                b = s - 5
                if live(b, looped):
                    dve.wait_ge(f2_ps, b + o + 1)
                    dve.wait_ge(xb_ok, b + o + 1)
                    if b >= 2:
                        dve.wait_ge(gate_ok, b + o - 1)
                    nc.vector.tensor_tensor(z[:, b % 2, :, :], bank[4 + b % 2][:, 0:TB * D].rearrange("p (j d) -> p j d", j=TB),
                                            xb[:, b % 2, :, :], ALU.add).then_inc(z_ok, 1)
                b = s - 2
                if live(b, looped):
                    dve.wait_ge(xT_ps, b + o + 1)
                    if b >= 2:
                        dve.wait_ge(h_ps, b + o - 1)
                        dve.wait_ge(xT_kept, b + o - 1)
                    nc.vector.tensor_copy(xT[:, b % 2, :], bank[(0, 6)[b % 2]][:, 0:T]).then_inc(xT_ok, 1)
                b = s
                if live(b, looped):
                    c = b % CYC
                    dve.wait_ge(x1_ld[c], 16 * (uses(b, w, CYC) + 1))
                    if b >= CYC:
                        dve.wait_ge(eps_add, b + o - CYC + 1)
                    made = count(dve, b + o + 1, looped)
                    for j in range(TB):
                        last = nc.vector.bn_stats(stats[:, b % 2, j, :], x_in[:, c, j, :])
                    last.then_inc(bn_st, 1)
                b = s - 3
                if live(b, looped):
                    dve.wait_ge(v_hi_ok, b + o + 1)
                    store = v_all[:, bass.ds(b + o, 1), :, :, :].rearrange("p o j g w -> p (o j) g w")
                    nc.vector.tensor_tensor(store[:, :, :, VW:VW + L],
                                            bank[(1, 7)[b % 2]][:, 0:TB * G * L].rearrange("p (j g l) -> p j g l", j=TB, g=G),
                                            store[:, :, :, 0:L], ALU.subtract).then_inc(v_kept, 1)
                b = s
                if live(b, looped):
                    c = b % CYC
                    dve.wait_ge(dve_const, 1)
                    dve.wait_ge(bn_st, made)
                    for j in range(TB):
                        last = nc.vector.bn_aggr(mv[:, c, j, :], stats[:, b % 2, j, :])
                    last.then_inc(bn_ag, 1)

            run(dve, step1, LAGS1, FIRST1)

            def step2(s, o, w, looped):
                def remainder(b, t):
                    if b >= 2:
                        dve.wait_ge(pv_ps, H * TB * (b + o - 1))
                    dve.wait_ge(p_hi_ok, PU * (b + o) + t + 1)
                    nc.vector.tensor_tensor(p_lo[:, b % 2, t, :], probs[:, t, :], p_hi[:, b % 2, t, :], ALU.subtract).then_inc(lo_dve, 1)

                def maxima(b, u):
                    blk, pair = u // 4, u % 4
                    if u == 0 and b >= 2:
                        dve.wait_ge(mT_ps, b + o - 1)
                    dve.wait_ge(s_ps, SU * (b + o) + u + 1)
                    keys = 128 * (blk + 1)
                    nc.vector.tensor_reduce(neg_max[:, b % 2, blk, 2 * pair:2 * pair + 2],
                                            bank[2 + u % 2][:, :].rearrange("p (h k) -> p h k", h=2)[:, :, 0:keys],
                                            AX.X, ALU.max, negate=True).then_inc(max_ok, 1)

                def divide(b, blk):
                    dve.wait_ge(pv_ps, H * TB * (b + o) + (12, 16)[blk])
                    if blk == 0 and b >= 2:
                        dve.wait_ge(yT_ps, b + o - 1)
                    y = bank[(1, 6)[blk]][:, 0:H * VW].rearrange("p (h w) -> p h w", h=H)
                    nc.vector.reciprocal(rden[:, b % 2, blk, :], y[:, :, L]).then_inc(rden_ok, 1)
                    dve.wait_ge(rden_ok, TB * (b + o) + blk + 1)
                    nc.vector.tensor_tensor(yn[:, b % 2, blk, :, :], y[:, :, 0:L],
                                            rden[:, b % 2, blk, :, None].to_broadcast([128, H, L]), ALU.mult).then_inc(yn_ok, 1)

                for u in range(SU):
                    if live(s - 2, looped):
                        maxima(s - 2, u)
                    if u == 0 and live(s - 5, looped):
                        divide(s - 5, 1)
                    b = s - 6
                    if u == 0 and live(b, looped):
                        dve.wait_ge(s_out, b + o + 1)
                        if b >= 2:
                            dve.wait_ge(res_ok, b + o - 1)
                        nc.vector.tensor_tensor(sg[:, b % 2, :, :], bank[7][:, 0:TB * D].rearrange("p (j d) -> p j d", j=TB),
                                                gate_all[:, bass.ds(b + o, 1), :, :].rearrange("p o j d -> p (o j) d"),
                                                ALU.mult).then_inc(sg_ok, 1)
                    b = s
                    if u == 2 and live(b, looped):
                        if b >= 2:
                            dve.wait_ge(q_stacked[(b - 2) % CYC], STACK_DMAS * (uses(b - 2, w, CYC) + 1))
                        dve.wait_ge(q_hi_ok, b + o + 1)
                        nc.vector.tensor_tensor(q_lo[:, b % 2, :, :], bank[0][:, :].rearrange("p (g t) -> p g t", g=G),
                                                q_hi[:, b % 2, :, :].bitcast(f32), ALU.subtract).then_inc(q_lo_ok, 1)
                    if u in (2, 3) and live(s - 4, looped):
                        remainder(s - 4, u + 1)
                    if u == 6 and live(b, looped):
                        dve.wait_ge(k_hi_ok, b + o + 1)
                        rows = slice(2 * L, 3 * L)
                        nc.vector.tensor_tensor(k_stack[rows, b % CYC, :, :], bank[0][rows, :].rearrange("p (g t) -> p g t", g=G),
                                                k_stack[rows, b % CYC, :, :].bitcast(f32), ALU.subtract).then_inc(k_lo_ok, 1)
                    if u == 6 and live(s - 4, looped):
                        divide(s - 4, 0)
                    if u in (6, 7) and live(s - 3, looped):
                        remainder(s - 3, u - 6)

            run(dve, step2, LAGS2, FIRST2)

        @block.tensor
        def _(pe):
            mm, tr = nc.tensor.matmul, nc.tensor.transpose
            pe.wait_ge(pool_const, 2)
            pe.wait_ge(ld_small, 64)
            tr(bank[7][:, 32:64], wup[:, 0, :], ident[0:L, 0:L])
            tr(bank[7][:, 64:96], wup[:, 1, :], ident[0:L, 0:L])
            tr(bank[7][:, 96:96 + E], b2_sb, ident[0:E, 0:E])
            for f in range(FB):
                last = tr(bank[7][:, 104 + E * f:104 + E * f + E], b1_sb[:, 128 * f:128 * f + 128], ident[0:E, 0:E])
            last.then_inc(small_T, 1)
            pe.wait_ge(last_step, 5)
            tr(bank[6][:, 32:32 + B], xnlast, ident[0:B, 0:B]).then_inc(last_T, 1)
            pe.wait_ge(last_cp, 1)
            mm(bank[6][:, 0:B], Wp1_sb, lastT, start=True, stop=True).then_inc(nav_ps, 1)
            pe.wait_ge(ld_wq, 16)
            for h in range(H):
                last = tr(bank[h // 4][:, 128 * (h % 4):128 * (h % 4) + 128], wq_sb[:, h, :], ident[:, :])
                if h % 4 == 3:
                    last.then_inc(wqT_ps, 1)
            pe.wait_ge(dve_const, 1)
            pe.wait_ge(nav_cp, 1)
            mm(bank[6][0:B, 64:64 + E], navT, Wp2_sb, start=True, stop=False)
            mm(bank[6][0:B, 64:64 + E], ones_row[:, 0:B], bp2_sb, start=False, stop=True).then_inc(lg_ps, 1)
            pe.wait_ge(ld_w2, 16)
            for i in range(E * FB):
                last = tr(bank[2 + i // 4][:, 128 * (i % 4):128 * (i % 4) + 128], W2_sb[:, i // FB, i % FB, :], ident[:, :])
                if i % 4 == 3:
                    last.then_inc(w2T_ps, 1)
            pe.wait_ge(sel_step, 4)
            mm(bank[6][0:1, 96:96 + B], selF, ident[0:B, 0:B], start=True, stop=True).then_inc(selT_ps, 1)
            pe.wait_ge(wqT_cp, 2)
            pe.wait_ge(tab_cp, 1)
            pe.wait_ge(rep_ok, 1)
            for g in range(G):
                last = tr(bank[7][:, 128 * g:128 * g + 128], wvd_rep[:, g, :, :].rearrange("p r l -> p (r l)"), ident[:, :])
            last.then_inc(wvT_ps, 1)
            for h in range(H):
                last = mm(bank[0][:, L * h:L * h + L], wqT[:, h, :], wupT[:, 0, :], start=True, stop=True)
            last.then_inc(A_ps, 1)
            pe.wait_ge(ld_wo, 48)
            for h in range(H):
                r, g = h % R, h // R
                last = mm(bank[1][L * r:L * r + L, D * g:D * g + D], wupT[:, 1, :], wo_sb[:, h, :], start=True, stop=True)
            last.then_inc(U_ps, 1)
            for i in range(E * FB):
                if i % 4 == 0:
                    pe.wait_ge(w2T_cp, i // 4 + 1)
                last = mm(bank[2 + i // 4][:, 128 * (i % 4):128 * (i % 4) + 128], W2T[:, i // FB, i % FB, :], Wo_sb, start=True, stop=True)
                if i % 4 == 3:
                    last.then_inc(w2o_ps, 1)
            pe.wait_ge(wv_step, 4)
            for g in range(G):
                last = tr(bank[7][:, 256 + L * g:256 + L * g + L], wvdT[:, g, :], ident[0:L, 0:L])
            last.then_inc(wvd_ps, 1)
            pe.wait_ge(wvd_ok, 1)
            pe.wait_ge(sel_ready, 1)
            for e in range(E):
                at = bank[6 + e // 4][:, 128 * (e % 4):128 * (e % 4) + 128]
                mm(at, b2rep[:, e, :], Wo_sb, start=True, stop=False)
                last = mm(at, ones_row[:, :], bo_sb, start=False, stop=True)
                if e % 4 == 3:
                    last.then_inc(b2o_ps, 1)
            pe.wait_ge(A_cp, 1)
            pe.wait_ge(U_cp, 1)
            pe.wait_ge(tab_cp, 7)
            pe.wait_ge(ld_w1, 48)

            def step1(s, o, w, looped):
                b = s - 4
                if live(b, looped):
                    pe.wait_ge(h_ok, b + o + 1)
                    if b >= 2:
                        pe.wait_ge(z_ok, b + o - 1)
                    for j in range(TB):
                        for f in range(FB):
                            last = mm(bank[4 + b % 2][:, D * j:D * j + D], hT[:, b % 2, f, 128 * j:128 * j + 128],
                                      wsel[:, b % CYC, W2O_AT + D * f:W2O_AT + D * f + D], start=(f == 0), stop=(f == FB - 1))
                    last.then_inc(f2_ps, 1)
                b = s - 2
                if live(b, looped):
                    pe.wait_ge(xn_ok, b + o + 1)
                    if b >= 2:
                        pe.wait_ge(xT_ok, b + o - 1)
                    for j in range(TB):
                        last = tr(bank[(0, 6)[b % 2]][:, 128 * j:128 * j + 128], xn[:, b % CYC, j, :], ident[:, :])
                    last.then_inc(xT_ps, 1)
                b = s - 3
                if live(b, looped):
                    c = b % CYC
                    pe.wait_ge(xT_ok, b + o + 1)
                    if b >= 2:
                        pe.wait_ge(v_kept, b + o - 1)
                    for j in range(TB):
                        last = mm(bank[(1, 7)[b % 2]][:, G * L * j:G * L * (j + 1)], xT[:, b % 2, 128 * j:128 * j + 128], wvd[:, :],
                                  start=True, stop=True)
                    last.then_inc(v_ps, 1)
                    pe.wait_ge(wsel_ld[c], 16 * (uses(b, w, CYC) + 1))
                    if b >= 2:
                        pe.wait_ge(h_ok, b + o - 1)
                    for f in range(FB):
                        last = mm(bank[2 + b % 2][:, T * f:T * f + T], wsel[:, c, W1_AT + 128 * f:W1_AT + 128 * f + 128], xT[:, b % 2, :],
                                  start=True, stop=True)
                    last.then_inc(h_ps, 1)

            run(pe, step1, LAGS1, FIRST1)
            pe.wait_ge(xT_kept, B)
            pe.wait_ge(v_kept, B)
            pe.wait_ge(h_ok, B)
            pe.wait_ge(z_ok, B)

            def step2(s, o, w, looped):
                xnT = xnT_all[:, bass.ds(s + o, 1), :].rearrange("p o t -> p (o t)") if live(s, looped) else None

                def keys(b):
                    pe.wait_ge(q_lo_ok, b + o + 1)
                    for g in range(G):
                        last = mm(bank[0][0:KR, T * g:T * g + T], WK3[:, g, :, :].rearrange("p r l -> p (r l)"), xnT, start=True, stop=True)
                    last.then_inc(k_ps, 1)

                def queries(b):
                    if b >= 3:
                        pe.wait_ge(m_row_ok, b + o - 2)
                    elif b >= 1:
                        pe.wait_ge(k_lo_ok, b + o)
                    for g in range(G):
                        last = mm(bank[0][:, T * g:T * g + T], A[:, 128 * g:128 * g + 128], xnT, start=True, stop=True)
                    last.then_inc(q_ps, 1)

                def transposed(b):
                    pe.wait_ge(yn_ok, TB * (b + o + 1))
                    if b >= 1:
                        pe.wait_ge(sg_ok, b + o)
                    for g in range(G):
                        for j in range(TB):
                            last = tr(bank[7][:, T * g + 128 * j:T * g + 128 * j + 128],
                                      yn[:, b % 2, j, R * g:R * g + R, :].rearrange("p h l -> p (h l)"), ident[:, :])
                    last.then_inc(yT_ps, 1)

                def projected(b):
                    pe.wait_ge(yT_ok, b + o + 1)
                    for j in range(TB):
                        for g in range(G):
                            last = mm(bank[7][:, D * j:D * j + D], yT[:, g, 128 * j:128 * j + 128], U[:, g, :], start=(g == 0), stop=(g == G - 1))
                    last.then_inc(s_out, 1)

                def scores(b, u):
                    c, blk, pair = b % CYC, u // 4, u % 4
                    if u == 0:
                        pe.wait_ge(q_stacked[c], STACK_DMAS * (uses(b, w, CYC) + 1))
                        pe.wait_ge(k_lo_ok, b + o + 1)
                    if SU * b + u >= 2:
                        pe.wait_ge(max_ok, SU * (b + o) + u - 1)
                    at = bank[2 + u % 2]
                    for i in range(2):
                        h = 2 * pair + i
                        mm(at[:, T * i:T * i + T], q_stack[0:KR, c, h, 128 * blk:128 * blk + 128], k_stack[0:KR, c, h // R, :],
                           start=(i == 0), stop=False)
                    mm(at[:, :].rearrange("p (h k) -> p h k", h=2)[:, :, 128 * blk:128 * blk + 128], identb[:, :], causal[:, :, :],
                       start=False, stop=True).then_inc(s_ps, 1)

                def maxima_by_head(b):
                    pe.wait_ge(max_ok, SU * (b + o + 1))
                    if looped or b + 2 < B:
                        pe.wait_ge(k_lo_ok, b + o + 3)
                    if b >= 1:
                        pe.wait_ge(m_row_ok, b + o)
                    for j in range(TB):
                        last = tr(bank[0][0:H, 128 * j:128 * j + 128], neg_max[:, b % 2, j, :], ident[:, :])
                    last.then_inc(mT_ps, 1)

                def shifted(b, t):
                    c, g, part = b % CYC, t // 3, t % 3
                    if t == 0:
                        pe.wait_ge(m_stacked[b % 2], 16 * (uses(b, w, 2) + 1))
                    if PU * b + t >= 2:
                        pe.wait_ge(exp_ok, PU * (b + o) + t - 1)
                    kb = part // 2
                    if kb == 0:
                        q = q_stack[0:KM, c, R * g + 2 * part:R * g + 2 * part + 2, :]
                    else:
                        q = q_stack[0:KM, c, R * g:R * g + R, 128:256]
                    mm(bank[4 + t % 2][:, :], k_stack[0:KM, c, g, 128 * kb:128 * kb + 128], q, start=True, stop=True).then_inc(st_ps, 1)

                def weighted(b, blk, h):
                    c, g, r = b % 2, h // R, h % R
                    if g == 0 and r == 0:
                        if blk == 0:
                            pe.wait_ge(vw_ld[c], 16 * (uses(b, w, 2) + 1))
                        if b >= 1:
                            pe.wait_ge(yn_ok, TB * (b + o) - 1 + blk)
                    if r % 2 == 0:
                        if blk == 0:
                            pe.wait_ge(lo_dve, 4 * (b + o) + 2 * g + r // 2 + 1)
                        elif r == 0:
                            pe.wait_ge(lo_pool, 2 * (b + o) + g + 1)
                    at = bank[(1, 6)[blk]][:, VW * h:VW * h + VW]
                    pieces = [(3 * g + r // 2, T * (r % 2) + 128 * blk, 0)]
                    if blk == 1:
                        pieces.append((3 * g + 2, 128 * r, 1))
                    for n, (t, off, kb) in enumerate(pieces):
                        v_lead, v_rest = v_w[:, c, kb, g, 0:VW], v_w[:, c, kb, g, VW:VW + L]
                        hi, lo = p_hi[:, c, t, off:off + 128], p_lo[:, c, t, off:off + 128]
                        mm(at, hi, v_lead, start=(n == 0), stop=False)
                        mm(at[:, 0:L], hi, v_rest, start=False, stop=False)
                        last = mm(at, lo, v_lead, start=False, stop=(n == len(pieces) - 1))
                    last.then_inc(pv_ps, 1)

                for u in range(SU):
                    if live(s - 2, looped):
                        scores(s - 2, u)
                    if live(s - 4, looped):
                        for r in (2 * (u % 2), 2 * (u % 2) + 1):
                            weighted(s - 4, u // 2 % 2, R * (u // 4) + r)
                    if u == 1 and live(s, looped):
                        queries(s)
                    if u == 3 and live(s - 5, looped):
                        transposed(s - 5)
                    if u >= 3 and live(s - 3, looped):
                        shifted(s - 3, u - 3)
                    if u == 4 and live(s, looped):
                        keys(s)
                if live(s - 5, looped):
                    projected(s - 5)
                if live(s - 3, looped):
                    shifted(s - 3, PU - 1)
                if live(s - 2, looped):
                    maxima_by_head(s - 2)

            run(pe, step2, LAGS2, FIRST2)


_INS = ["L0_attn_x", "L0_attn_wq", "L0_attn_wk_down", "L0_attn_wv_down", "L0_attn_wk_up", "L0_attn_wv_up", "L0_attn_wo",
        "L0_ffn_Wp1", "L0_ffn_bp1", "L0_ffn_Wp2", "L0_ffn_bp2", "L0_ffn_W1", "L0_ffn_b1", "L0_ffn_W2", "L0_ffn_b2",
        "L0_ffn_Wo", "L0_ffn_bo"]


def kernel(**inputs):
    import concourse.bacc as bacc
    from concourse.bass_utils import run_bass_kernel_spmd

    nc = bacc.Bacc("TRN2", target_bir_lowering=False, num_devices=1)
    arrays, args = {}, []
    for name in _INS:
        a = np.ascontiguousarray(inputs[name])
        arrays[name] = a
        args.append(nc.dram_tensor(name, a.shape, mybir.dt.from_np(a.dtype), kind="ExternalInput").ap())
    shape = arrays["L0_attn_x"].shape
    args.append(nc.dram_tensor("out", shape, mybir.dt.float32, kind="ExternalOutput").ap())
    layernorm_mla_attention_times_routed_ffn_gate(nc, *args)
    return run_bass_kernel_spmd(nc, [arrays], core_ids=[0]).results[0]["out"]
```

```python
import concourse.bass as bass
from concourse import mybir
from contextlib import ExitStack
import numpy as np


def layernorm_mla_attention_times_routed_ffn_gate(
    nc, x, wq, wk_down, wv_down, wk_up, wv_up, wo,
    Wp1, bp1, Wp2, bp2, W1, b1, W2, b2, Wo, bo, out,
):
    f32, f32r, bf16, f16 = mybir.dt.float32, mybir.dt.float32r, mybir.dt.bfloat16, mybir.dt.float16
    i32, u32 = mybir.dt.int32, mybir.dt.uint32
    ALU, ACT, AX = mybir.AluOpType, mybir.ActivationFunctionType, mybir.AxisListType

    B, T, D = x.shape
    L = wk_up.shape[0]
    G = wk_down.shape[1] // L
    HD = wk_up.shape[1]
    H = wq.shape[1] // HD
    R = H // G
    E, _, F = W1.shape
    FB, TB = F // 128, T // 128
    VW = L + 1
    VP = 2 * L + 2
    SCALE = float(HD) ** -0.5
    MASKED = -1e30
    EPS = 1e-5
    W1_AT, W2O_AT, B2O_AT, B1_AT = 0, F, 2 * F, 2 * F + D
    EW = B1_AT + FB
    KR = 3 * L
    KM = KR + 1
    SU = 8
    PU = 6
    CYC = 4

    ctx = ExitStack()
    with ctx:
        def sb(name, shape, dt=f32):
            return ctx.enter_context(nc.sbuf_tensor(name, shape, dt))

        def sem(name):
            return ctx.enter_context(nc.semaphore(name))

        xnT_all = sb("xnT_all", [128, B, T])
        gate_all = sb("gate_all", [128, B, TB, D])
        v_all = sb("v_all", [128, B, TB, G, VP], f16)
        A = sb("A", [128, H * L])
        wkd = sb("wkd", [128, G * L])
        wvd = sb("wvd", [128, G * L])
        U = sb("U", [128, G, D])
        ident = sb("ident", [128, 128])
        identb = sb("identb", [128, 128], bf16)
        causal = sb("causal", [128, 2, 128], bf16)
        ones_row = sb("ones_row", [1, 128])
        neg_half = sb("neg_half", [128, TB])
        sel_row = sb("sel_row", [1, B], i32)
        BIG = (2 + 1) * PU * 512
        big = sb("big", [128, BIG])
        table = big[:, 0:E * EW].rearrange("p (e w) -> p e w", e=E)
        o = E * EW
        wsel = big[:, o:o + CYC * EW].rearrange("p (c w) -> p c w", c=CYC)
        o += CYC * EW
        hT = big[:, o:o + 2 * FB * T].rearrange("p (c f t) -> p c f t", c=2, f=FB)
        o += 2 * FB * T
        assert o <= BIG
        parts = big[:, 0:2 * PU * 512].bitcast(f16).rearrange("p (i c u n) -> p i c u n", i=2, c=2, u=PU)
        p_hi, p_lo = parts[:, 0, :, :, :], parts[:, 1, :, :, :]
        probs = big[:, 2 * PU * 512:BIG].rearrange("p (u n) -> p u n", u=PU)
        flat = gate_all[:, :, :, :].rearrange("p b j d -> p (b j d)")
        W2T = flat[:, 0:2048].rearrange("p (e f j) -> p e f j", e=E, f=FB)
        wqT = flat[:, 2048:3072].rearrange("p (h d) -> p h d", h=H)
        b2rep = flat[:, 3072:4096].rearrange("p (e j) -> p e j", e=E)
        flat2 = xnT_all[:, :, :].rearrange("p b t -> p (b t)")
        W2_sb = flat2[:, 0:2048].rearrange("p (e f h) -> p e f h", e=E, f=FB)
        wq_sb = flat2[:, 2048:3072].rearrange("p (h d) -> p h d", h=H)
        wo_sb = flat2[:, 3072:4096].rearrange("p (h d) -> p h d", h=H)
        Wo_sb = flat2[:, 4096:4224]
        wup = flat2[0:L, 4224:4480].rearrange("l (k d) -> l k d", k=2)
        b1_sb = flat2[0:E, 4480:4736]
        b2_sb = flat2[0:E, 4736:4864]
        bo_sb = flat2[0:1, 4864:4992]
        Wp1_sb = flat2[:, 4992:5120]
        Wp2_sb = flat2[:, 5120:5128]
        bp1_sb = flat2[:, 5128:5129]
        bp2_sb = flat2[0:1, 5136:5144]
        xlast = flat2[0:B, 5248:5376]
        xnlast = flat2[0:B, 5376:5504]
        lastT = flat2[:, 5504:5504 + B]
        navT = flat2[:, 5536:5536 + B]
        logits = flat2[0:B, 5568:5576]
        top8 = flat2[0:B, 5576:5584]
        wupT = flat2[:, 5600:5664].rearrange("p (k l) -> p k l", k=2)
        st_last = flat2[0:B, 5664:5670]
        mv_last = flat2[0:B, 5672:5674]
        rs_last = flat2[0:B, 5674:5675]
        selF = flat2[0:B, 5675:5676]
        wvd_in = flat2[:, 5680:5744].rearrange("p (g l) -> p g l", g=G)
        wvd_rep = flat2[:, 5744:6000].rearrange("p (g r l) -> p g r l", g=G, r=R)
        wvdT = flat2[0:L, 6000:6256].rearrange("l (g d) -> l g d", g=G)
        col_max = flat2[:, 6256:6256 + G]
        col_rcp = flat2[:, 6258:6258 + G]
        sel_idx = sb("sel_idx", [B, 8], u32)
        x_in = sb("x_in", [128, CYC, TB, D])
        xn = sb("xn", [128, CYC, TB, D])
        xT = sb("xT", [128, 2, T])
        stats = sb("stats", [128, 2, TB, 6])
        mv = sb("mv", [128, CYC, TB, 2])
        var_eps = sb("var_eps", [128, 2, TB])
        rstd = sb("rstd", [128, CYC, TB])
        xb = sb("xb", [128, 2, TB, D])
        zth = sb("zth", [128, CYC, TB, D])
        z, th = zth[:, 0:2, :, :], zth[:, 2:4, :, :]
        q_hi = sb("q_hi", [128, CYC, G, T], f32r)
        q_lo = sb("q_lo", [128, CYC, G, T], f32r)
        k_parts = sb("k_parts", [G * L, 2, CYC, T], f32r)
        q_stack = sb("q_stack", [128, R, CYC, G, T], f32r)
        k_stack = sb("k_stack", [128, G, CYC, T], f32r)
        neg_max = sb("neg_max", [128, 2, TB, H])
        m_row = sb("m_row", [H, T], f32r)
        v_w = sb("v_w", [128, CYC, TB, G, VP], f16)
        rden = sb("rden", [128, 2, TB, H])
        yn = xn[:, :, :, :].rearrange("p (c e) j d -> p c (e j d)", c=2).rearrange("p c (j h l) -> p c j h l", j=TB, h=H)
        yT = xT
        sg = xb
        res = zth

        bank = [ctx.enter_context(nc.psum_tensor(f"bank{i}", [128, 512], f32)) for i in range(8)]

        ld_router, ld_small, ld_wq, ld_w2 = sem("ld_router"), sem("ld_small"), sem("ld_wq"), sem("ld_w2")
        ld_wo, ld_w1, ld_wvd = sem("ld_wo"), sem("ld_w1"), sem("ld_wvd")
        pool_set, pool_const = sem("pool_set"), sem("pool_const")
        dve_const = sem("dve_const")
        last_step = sem("last_step")
        small_T, small_cp = sem("small_T"), sem("small_cp")
        last_T, last_cp = sem("last_T"), sem("last_cp")
        nav_ps, nav_cp = sem("nav_ps"), sem("nav_cp")
        lg_ps, sel_step = sem("lg_ps"), sem("sel_step")
        selT_ps, sel_ready = sem("selT_ps"), sem("sel_ready")
        wqT_ps, wqT_cp = sem("wqT_ps"), sem("wqT_cp")
        w2T_ps, w2T_cp = sem("w2T_ps"), sem("w2T_cp")
        A_ps, U_ps, w2o_ps, b2o_ps = sem("A_ps"), sem("U_ps"), sem("w2o_ps"), sem("b2o_ps")
        A_cp, U_cp, tab_cp = sem("A_cp"), sem("U_cp"), sem("tab_cp")
        rep_ok, wvT_ps, wv_step, wvd_ps, wvd_ok = sem("rep_ok"), sem("wvT_ps"), sem("wv_step"), sem("wvd_ps"), sem("wvd_ok")
        bn_st, bn_ag = sem("bn_st"), sem("bn_ag")
        x1_ld = [sem(f"x1_ld{c}") for c in range(CYC)]
        eps_add, rstd_ok, xn_ok = sem("eps_add"), sem("rstd_ok"), sem("xn_ok")
        xT_ps, xT_ok, xT_kept, xb_ok = sem("xT_ps"), sem("xT_ok"), sem("xT_kept"), sem("xb_ok")
        wsel_ld = [sem(f"wsel_ld{c}") for c in range(CYC)]
        v_ps, v_hi_ok, v_kept, h_ps, h_ok, f2_ps, z_ok = (sem(n) for n in (
            "v_ps", "v_hi_ok", "v_kept", "h_ps", "h_ok", "f2_ps", "z_ok"))
        th_ok, gate_ok = sem("th_ok"), sem("gate_ok")
        k_ps, q_ps, k_hi_ok, q_hi_ok, k_lo_ok, q_lo_ok = (sem(n) for n in (
            "k_ps", "q_ps", "k_hi_ok", "q_hi_ok", "k_lo_ok", "q_lo_ok"))
        m_stacked = [[sem(f"m_stacked{c}{g}") for g in range(G)] for c in range(2)]
        k_stacked = [sem(f"k_stacked{c}") for c in range(CYC // 2)]
        q_stacked = [[sem(f"q_stacked{c}{i}") for i in range(2)] for c in range(CYC // 2)]
        s_ps, max_ok, mT_ps, m_row_ok = (sem(n) for n in ("s_ps", "max_ok", "mT_ps", "m_row_ok"))
        st_ps, exp_ok, causal_ok = sem("st_ps"), sem("exp_ok"), sem("causal_ok")
        p_hi_ok, lo_dve, lo_pool = sem("p_hi_ok"), sem("lo_dve"), sem("lo_pool")
        vw_ld = [sem(f"vw_ld{c}") for c in range(2)]
        pv_ps, rden_ok, yn_ok = sem("pv_ps"), sem("rden_ok"), sem("yn_ok")
        yT_ps, yT_ok, s_out, sg_ok, res_ok = (sem(n) for n in ("yT_ps", "yT_ok", "s_out", "sg_ok", "res_ok"))
        x2_ld = [sem(f"x2_ld{c}") for c in range(2)]
        out_st = [sem(f"out_st{c}") for c in range(2)]

        block = ctx.enter_context(nc.Block())

        Q_STACK_DMAS = R * 16
        K_STACK_DMAS = 2 * G * 16
        x_v = x.rearrange("b (j p) d -> b p j d", p=128)
        out_v = out.rearrange("b (j p) d -> b p j d", p=128)

        def run(eng, step, lags, first, lead=0, begun=0, left=0):
            turns = (B - lead - first) // CYC
            for s in range(begun, first):
                step(s, 0, 0, False)
            with eng.Fori(0, turns) as i:
                for s in range(first, first + CYC):
                    step(s, i * CYC, i, True)
            for s in range(first + turns * CYC, B + lags - left):
                step(s, 0, 0, False)

        def join(step1, step2):
            for k in range(JOINED):
                step1(B + LAGS1 - JOINED + k, 0, 0, False)
                step2(k, 0, 0, False)

        JOINED = 5
        LAGS1, FIRST1 = 6, 10
        LAGS2, FIRST2 = 9, 10

        def uses(b, w, n):
            return b // n + (CYC // n) * w

        def count(eng, n, looped):
            return eng.snap(eng.to_reg(n)) if looped else n

        def remainder_of(t):
            return (lo_dve, (0, 1, 3).index(t) + 1) if t in (0, 1, 3) else (lo_pool, (2, 4, 5).index(t) + 1)

        PAIRS = (0, 2, 1, 3)

        def k_buf(b):
            return (b + 1) % CYC

        def live(b, looped):
            return looped or 0 <= b < B

        @block.sync
        def _(sp):
            ld = sp.dma_start
            ld(xlast, x[:, T - 1, :]).then_inc(ld_router, 16)
            ld(Wp1_sb, Wp1).then_inc(ld_router, 16)
            ld(bp1_sb, bp1.rearrange("(n o) -> n o", o=1)).then_inc(ld_router, 16)
            ld(Wp2_sb, Wp2).then_inc(ld_router, 16)
            ld(bp2_sb, bp2.rearrange("(o n) -> o n", o=1)).then_inc(ld_router, 16)
            ld(wup[:, 0, :], wk_up).then_inc(ld_small, 16)
            ld(wup[:, 1, :], wv_up).then_inc(ld_small, 16)
            ld(b1_sb, b1).then_inc(ld_small, 16)
            ld(b2_sb, b2).then_inc(ld_small, 16)
            ld(wvd_in, wv_down.rearrange("p (g l) -> p g l", g=G)).then_inc(ld_wvd, 16)
            ld(wq_sb, wq.rearrange("p (h d) -> p h d", h=H)).then_inc(ld_wq, 16)
            ld(W2_sb, W2.rearrange("e (f p) h -> p e f h", p=128)).then_inc(ld_w2, 16)
            def load_x(b, o, done, c):
                sp.dma_start(x_in[:, c, :, :], x_v[bass.ds(b + o, 1), :, :, :].rearrange("o p j d -> p (o j) d")).then_inc(done[c], 16)

            load_x(0, 0, x1_ld, 0)
            ld(Wo_sb, Wo).then_inc(ld_wo, 16)
            ld(bo_sb, bo.rearrange("(o n) -> o n", o=1)).then_inc(ld_wo, 16)
            ld(wo_sb, wo.rearrange("(h p) o -> p h o", p=128)).then_inc(ld_wo, 16)
            ld(table[:, :, W1_AT:W1_AT + F], W1.rearrange("e p f -> p e f")).then_inc(ld_w1, 16)
            ld(wkd[:, :], wk_down).then_inc(ld_w1, 16)

            load_x(1, 0, x1_ld, 1)

            def step1(s, o, w, looped):
                b = s + 2
                if live(b, looped):
                    c = b % CYC
                    sp.wait_ge(ld_router, 80)
                    if b >= CYC:
                        sp.wait_ge(xn_ok, b + o - CYC + 1)
                    load_x(b, o, x1_ld, c)
                b = s - 1
                if live(b, looped):
                    c = b % CYC
                    if b == 0:
                        for q in (tab_cp, 7), (ld_w1, 32), (sel_ready, 1):
                            sp.wait_ge(*q)
                    expert = sp.value_load(sel_row[0:1, bass.ds(b + o, 1)], min_val=0, max_val=E - 1)
                    sp.wait_ge(ld_router, 80)
                    if b >= CYC:
                        sp.wait_ge(f2_ps, b + o - CYC + 1)
                        sp.wait_ge(h_ok, b + o - CYC + 1)
                        sp.wait_ge(xb_ok, b + o - CYC + 1)
                    sp.dma_start(wsel[:, c, :], table[:, bass.ds(expert, 1), :].rearrange("p o w -> p (o w)")).then_inc(wsel_ld[c], 16)

            run(sp, step1, LAGS1, FIRST1, lead=2)

            def step2(s, o, w, looped):
                def stack_max(g):
                    b = s - 4
                    if live(b, looped):
                        if g == 0:
                            sp.wait_ge(m_row_ok, b + o + 1)
                        sp.dma_start(q_stack[KR:KM, :, b % CYC, g, :].bitcast(f32),
                                     m_row[R * g:R * g + R, :].bitcast(f32)).then_inc(m_stacked[b % 2][g], 16)

                stack_max(0)
                pair = s - 2
                if s % 2 == 0 and live(pair, looped):
                    c = pair % CYC
                    made = count(sp, pair + o + 2, looped)
                    if pair >= CYC:
                        sp.wait_ge(st_ps, PU * (pair + o - 2))
                    sp.wait_ge(q_hi_ok, made)
                    sp.wait_ge(q_lo_ok, made)
                    for r in range(R):
                        if r == 2:
                            stack_max(1)
                        done = q_stacked[c // 2][r // 2]
                        sp.dma_start(q_stack[0:2 * L, r, c:c + 2, :, :].bitcast(f32),
                                     q_hi[r * L:r * L + L, None, c:c + 2, :, :].to_broadcast([L, 2, 2, G, T]).bitcast(f32)).then_inc(done, 16)
                        sp.dma_start(q_stack[2 * L:3 * L, r, c:c + 2, :, :].bitcast(f32),
                                     q_lo[r * L:r * L + L, c:c + 2, :, :].bitcast(f32)).then_inc(done, 16)
                else:
                    stack_max(1)
                if s % 2 == 1:
                    seqs = [b for b in (s - 2, s - 1) if live(b, looped)]
                    if seqs:
                        c, n = k_buf(seqs[0]), len(seqs)
                        made = count(sp, seqs[-1] + o + 1, looped)
                        if seqs[-1] >= CYC:
                            sp.wait_ge(st_ps, PU * (seqs[-1] + o - CYC + 1))
                        sp.wait_ge(k_lo_ok, made)
                        for g in range(G):
                            rows = slice(g * L, g * L + L)
                            sp.dma_start(k_stack[0:2 * L, g, c:c + n, :].bitcast(f32),
                                         k_parts[rows, :, c:c + n, :].bitcast(f32)).then_inc(k_stacked[c // 2], 16)
                            sp.dma_start(k_stack[2 * L:3 * L, g, c:c + n, :].bitcast(f32),
                                         k_parts[rows, 0, c:c + n, :].bitcast(f32)).then_inc(k_stacked[c // 2], 16)
                b = s - 3
                if s % 2 and live(b, looped):
                    c = b % CYC
                    sp.wait_ge(ld_router, 80)
                    if b == 0:
                        sp.wait_ge(v_kept, B)
                    if b >= CYC:
                        sp.wait_ge(pv_ps, H * TB * (b + o - 2))
                    sp.dma_start(v_w[:, c:c + 2, :, :, :].rearrange("p e j g w -> p e (j g w)"),
                                 v_all[:, bass.ds(b + o, 2), :, :, :].rearrange("p e j g w -> p e (j g w)")).then_inc(vw_ld[c // 2], 16)
                b = s - 5
                if s % 2 and live(b, looped):
                    c = b % CYC
                    sp.wait_ge(ld_router, 80)
                    if b >= CYC:
                        sp.wait_ge(res_ok, b + o - 2)
                    elif b == 0:
                        sp.wait_ge(xn_ok, B)
                    sp.dma_start(x_in[:, c:c + 2, :, :], x_v[bass.ds(b + o, 2), :, :, :].rearrange("e p j d -> p e j d")).then_inc(x2_ld[c // 2], 16)
                b = s - 9
                if s % 2 and live(b, looped):
                    c = b % CYC
                    sp.wait_ge(ld_router, 80)
                    sp.wait_ge(res_ok, b + o + 2)
                    sp.dma_start(out_v[bass.ds(b + o, 2), :, :, :].rearrange("e p j d -> p e j d"), res[:, c:c + 2, :, :]).then_inc(out_st[c // 2], 16)

            run(sp, step2, LAGS2, FIRST2)
            for c in range(2):
                sp.wait_ge(out_st[c], 16 * (B // CYC))

        @block.gpsimd
        def _(pool):
            nc.gpsimd.memset(ident[:, :], 0.0).then_inc(pool_set, 1)
            nc.gpsimd.memset(causal[:, :, :], 0.0).then_inc(pool_set, 1)
            nc.gpsimd.memset(neg_half[:, :], -0.5)
            pool.wait_ge(pool_set, 1)
            nc.gpsimd.affine_select(out=ident[:, :], in_=ident[:, :], compare_op=ALU.not_equal, fill=1.0,
                                    base=0, pattern=[[-1, 128]], channel_multiplier=1).then_inc(pool_const, 1)
            pool.wait_ge(pool_set, 2)
            nc.gpsimd.affine_select(out=causal[:, :, :], in_=causal[:, :, :], compare_op=ALU.is_ge, fill=MASKED,
                                    base=0, pattern=[[0, 2], [-1, 128]], channel_multiplier=1)
            pool.wait_ge(pool_const, 1)
            nc.gpsimd.tensor_copy(identb[:, :], ident[:, :]).then_inc(pool_const, 1)
            pool.wait_ge(last_step, 2)
            nc.gpsimd.tensor_scalar(rs_last, mv_last[:, 1:2], EPS, None, ALU.add).then_inc(last_step, 1)
            pool.wait_ge(last_step, 3)
            nc.gpsimd.tensor_tensor(rs_last, rs_last, neg_half[0:B, 0:1], ALU.pow).then_inc(last_step, 1)
            pool.wait_ge(ld_wvd, 16)
            for r in range(R):
                last = nc.gpsimd.tensor_copy(wvd_rep[:, :, r, :], wvd_in)
            last.then_inc(rep_ok, 1)

            def step1(s, o, w, looped):
                b = s
                if live(b, looped):
                    c = b % CYC
                    made = count(pool, b + o + 1, looped)
                    pool.wait_ge(pool_const, 2)
                    pool.wait_ge(bn_ag, made)
                    nc.gpsimd.tensor_scalar(var_eps[:, b % 2, :], mv[:, c, :, 1], EPS, None, ALU.add).then_inc(eps_add, 1)
                    pool.wait_ge(eps_add, b + o + 1)
                    if b >= CYC:
                        pool.wait_ge(xn_ok, b + o - CYC + 1)
                    nc.gpsimd.tensor_tensor(rstd[:, c, :], var_eps[:, b % 2, :], neg_half[:, :], ALU.pow).then_inc(rstd_ok, 1)
                b = s - 4
                if live(b, looped):
                    c = b % CYC
                    pool.wait_ge(xn_ok, b + o + 1)
                    pool.wait_ge(wsel_ld[c], 16 * (uses(b, w, CYC) + 1))
                    if b >= 2:
                        pool.wait_ge(z_ok, b + o - 1)
                    for j in range(TB):
                        last = nc.gpsimd.tensor_tensor(xb[:, b % 2, j, :], xn[:, c, j, :], wsel[:, c, B2O_AT:B2O_AT + D], ALU.add)
                    last.then_inc(xb_ok, 1)

            run(pool, step1, LAGS1, FIRST1, left=JOINED)

            def step2(s, o, w, looped):
                def cut(b, t):
                    made = count(pool, PU * (b + o) + t + 1, looped)
                    pool.wait_ge(pool_const, 2)
                    pool.wait_ge(exp_ok, made)
                    if t % 3 < 2:
                        upper = probs[:, t, :].rearrange("p (h q) -> p h q", h=2)[:, :, 0:128]
                        heads = 2
                    else:
                        upper = probs[:, t, :].rearrange("p (h q) -> p h q", h=R)
                        heads = R
                    nc.gpsimd.affine_select(out=upper, in_=upper, compare_op=ALU.is_ge, fill=0.0, base=0,
                                            pattern=[[0, heads], [1, 128]], channel_multiplier=-1).then_inc(causal_ok, 1)

                def remainder(b, t):
                    pool.wait_ge(p_hi_ok, PU * (b + o) + t + 1)
                    if b >= 2:
                        pool.wait_ge(pv_ps, H * TB * (b + o - 1))
                    nc.gpsimd.tensor_tensor(p_lo[:, b % 2, t, :], probs[:, t, :], p_hi[:, b % 2, t, :], ALU.subtract).then_inc(lo_pool, 1)

                if live(s - 5, looped):
                    cut(s - 5, PU - 3)
                    cut(s - 5, PU - 2)
                    remainder(s - 5, 2)
                    cut(s - 5, PU - 1)
                b = s - 7
                if live(b, looped):
                    pool.wait_ge(sg_ok, b + o + 1)
                    pool.wait_ge(x2_ld[b % CYC // 2], 16 * (uses(b, w, CYC) + 1))
                    if b >= CYC:
                        pool.wait_ge(out_st[b % CYC // 2], 16 * uses(b, w, CYC))
                    nc.gpsimd.tensor_tensor(res[:, b % CYC, :, :], sg[:, b % 2, :, :], x_in[:, b % CYC, :, :], ALU.add).then_inc(res_ok, 1)
                if live(s - 5, looped):
                    remainder(s - 5, PU - 2)
                    remainder(s - 5, PU - 1)
                if live(s - 4, looped):
                    for t in range(PU - 3):
                        cut(s - 4, t)

            join(step1, step2)
            run(pool, step2, LAGS2, FIRST2, begun=JOINED)

        @block.scalar
        def _(act):
            act.wait_ge(nav_ps, 1)
            nc.scalar.activation(navT, bank[6][:, 0:B], ACT.Gelu, bias=bp1_sb).then_inc(nav_cp, 1)
            for i in range(2):
                act.wait_ge(wqT_ps, i + 1)
                nc.scalar.copy(wqT[:, 4 * i:4 * i + 4, :], bank[i][:, :].rearrange("p (h d) -> p h d", h=4)).then_inc(wqT_cp, 1)
            for i in range(4):
                act.wait_ge(w2T_ps, i + 1)
                nc.scalar.copy(flat[:, 512 * i:512 * i + 512], bank[2 + i][:, :]).then_inc(w2T_cp, 1)
            act.wait_ge(A_ps, 1)
            nc.scalar.mul(A[:, :], bank[0][:, 0:H * L], SCALE).then_inc(A_cp, 1)
            for i in range(4):
                act.wait_ge(w2o_ps, i + 1)
                nc.scalar.mul(table[:, 2 * i:2 * i + 2, W2O_AT:W2O_AT + F],
                              bank[2 + i][:, :].rearrange("p (e n) -> p e n", e=2), 0.3).then_inc(tab_cp, 1)

            def step1(s, o, w, looped):
                b = s - 3
                if live(b, looped):
                    if b == 0:
                        for q in (tab_cp, 7), (A_cp, 1), (U_cp, 1), (wvd_ok, 1), (selT_ps, 1):
                            act.wait_ge(*q)
                    act.wait_ge(xT_ok, b + o + 1)
                    nc.scalar.copy(xnT_all[:, bass.ds(b + o, 1), :].rearrange("p o t -> p (o t)"), xT[:, b % 2, :]).then_inc(xT_kept, 1)
                    act.wait_ge(v_ps, b + o + 1)
                    nc.scalar.copy(v_all[:, bass.ds(b + o, 1), :, :, 0:L].rearrange("p o j g l -> p (o j) g l"),
                                   bank[(1, 7)[b % 2]][:, 0:TB * G * L].rearrange("p (j g l) -> p j g l", j=TB, g=G)).then_inc(v_hi_ok, 1)
                b = s - 5
                if live(b, looped):
                    act.wait_ge(z_ok, b + o + 1)
                    if b >= 2:
                        act.wait_ge(gate_ok, b + o - 1)
                    nc.scalar.activation(th[:, b % 2, :, :], z[:, b % 2, :, :], ACT.Tanh, scale=0.5).then_inc(th_ok, 1)
                b = s - 3
                if live(b, looped):
                    if b >= 2:
                        act.wait_ge(f2_ps, b + o - 1)
                    act.wait_ge(wsel_ld[b % CYC], 16 * (uses(b, w, CYC) + 1))
                    act.wait_ge(h_ps, b + o + 1)
                    for f in range(FB):
                        last = nc.scalar.activation(hT[:, b % 2, f, :], bank[2 + b % 2][:, f * T:f * T + T], ACT.Gelu,
                                                    bias=wsel[:, b % CYC, B1_AT + f:B1_AT + f + 1])
                    last.then_inc(h_ok, 1)

            run(act, step1, LAGS1, FIRST1, left=JOINED)

            def step2(s, o, w, looped):
                def exponent(b, t):
                    if b == 0 and t == 0:
                        act.wait_ge(gate_ok, B)
                    if b >= 1:
                        done, n = remainder_of(t)
                        act.wait_ge(done, 3 * (b + o - 1) + n)
                    act.wait_ge(st_ps, PU * (b + o) + t + 1)
                    nc.scalar.activation(probs[:, t, :], bank[4 + t % 2][:, :], ACT.Exp).then_inc(exp_ok, 1)

                def leading(b, t):
                    if b >= 2:
                        act.wait_ge(pv_ps, H * TB * (b + o - 1))
                    act.wait_ge(causal_ok, PU * (b + o) + t + 1)
                    nc.scalar.copy(p_hi[:, b % 2, t, :], probs[:, t, :]).then_inc(p_hi_ok, 1)

                if live(s - 5, looped):
                    exponent(s - 5, PU - 2)
                b = s - 4
                if live(b, looped):
                    act.wait_ge(mT_ps, b + o + 1)
                    if b >= 1:
                        for done in m_stacked[(b - 1) % 2]:
                            act.wait_ge(done, 16 * (uses(b - 1, w, 2) + 1))
                    nc.scalar.copy(m_row[:, :], bank[0][0:H, 0:T]).then_inc(m_row_ok, 1)
                if live(s - 5, looped):
                    leading(s - 5, 2)
                    exponent(s - 5, 5)
                    leading(s - 5, 3)
                b = s
                if live(b, looped):
                    if b >= CYC:
                        for done in q_stacked[b % CYC // 2]:
                            act.wait_ge(done, Q_STACK_DMAS * uses(b, w, CYC))
                        act.wait_ge(q_lo_ok, b + o - CYC + 1)
                    act.wait_ge(q_ps, b + o + 1)
                    nc.scalar.copy(q_hi[:, b % CYC, :, :], bank[0][:, :].rearrange("p (g t) -> p g t", g=G)).then_inc(q_hi_ok, 1)
                if live(s - 5, looped):
                    leading(s - 5, 4)
                    leading(s - 5, 5)
                if live(s - 4, looped):
                    exponent(s - 4, 0)
                    exponent(s - 4, 1)
                if live(s - 4, looped):
                    exponent(s - 4, 2)
                    leading(s - 4, 0)
                b = s
                if live(b, looped):
                    c = k_buf(b)
                    if b + 1 >= CYC:
                        act.wait_ge(k_stacked[c // 2], K_STACK_DMAS * uses(b + 1, w, CYC))
                    act.wait_ge(k_ps, b + o + 1)
                    nc.scalar.copy(k_parts[:, 0, c, :], bank[0][0:G * L, 0:T]).then_inc(k_hi_ok, 1)
                if live(s - 4, looped):
                    exponent(s - 4, 3)
                b = s - 6
                if live(b, looped):
                    act.wait_ge(yT_ps, b + o + 1)
                    if b >= 1:
                        act.wait_ge(s_out, b + o)
                    nc.scalar.copy(yT[:, :, :], bank[7][:, :].rearrange("p (g t) -> p g t", g=G)).then_inc(yT_ok, 1)
                if live(s - 4, looped):
                    leading(s - 4, 1)

            join(step1, step2)
            run(act, step2, LAGS2, FIRST2, begun=JOINED)

        @block.vector
        def _(dve):
            def step1(s, o, w, looped):
                b = s
                if live(b, looped):
                    c = b % CYC
                    dve.wait_ge(x1_ld[c], 16 * (uses(b, w, CYC) + 1))
                    if b >= CYC:
                        dve.wait_ge(eps_add, b + o - CYC + 1)
                    made = count(dve, b + o + 1, looped)
                    for j in range(TB):
                        last = nc.vector.bn_stats(stats[:, b % 2, j, :], x_in[:, c, j, :])
                    last.then_inc(bn_st, 1)
                b = s - 5
                if live(b, looped):
                    dve.wait_ge(f2_ps, b + o + 1)
                    dve.wait_ge(xb_ok, b + o + 1)
                    if b >= 2:
                        dve.wait_ge(gate_ok, b + o - 1)
                    nc.vector.tensor_tensor(z[:, b % 2, :, :], bank[4 + b % 2][:, 0:TB * D].rearrange("p (j d) -> p j d", j=TB),
                                            xb[:, b % 2, :, :], ALU.add).then_inc(z_ok, 1)
                b = s
                if live(b, looped):
                    c = b % CYC
                    dve.wait_ge(dve_const, 1)
                    dve.wait_ge(bn_st, made)
                    for j in range(TB):
                        last = nc.vector.bn_aggr(mv[:, c, j, :], stats[:, b % 2, j, :])
                    last.then_inc(bn_ag, 1)
                b = s - 6
                if live(b, looped):
                    dve.wait_ge(th_ok, b + o + 1)
                    nc.vector.scalar_tensor_tensor(out=gate_all[:, bass.ds(b + o, 1), :, :].rearrange("p o j d -> p (o j d)"),
                                                   in0=th[:, b % 2, :, :].rearrange("p j d -> p (j d)"), scalar=1.0,
                                                   in1=z[:, b % 2, :, :].rearrange("p j d -> p (j d)"),
                                                   op0=ALU.add, op1=ALU.mult).then_inc(gate_ok, 1)
                b = s - 2
                if live(b, looped):
                    dve.wait_ge(xT_ps, b + o + 1)
                    if b >= 2:
                        dve.wait_ge(h_ps, b + o - 1)
                        dve.wait_ge(xT_kept, b + o - 1)
                    nc.vector.tensor_copy(xT[:, b % 2, :], bank[(0, 6)[b % 2]][:, 0:T]).then_inc(xT_ok, 1)
                b = s - 3
                if live(b, looped):
                    dve.wait_ge(v_hi_ok, b + o + 1)
                    store = v_all[:, bass.ds(b + o, 1), :, :, :].rearrange("p o j g w -> p (o j) g w")
                    nc.vector.tensor_tensor(store[:, :, :, VW:VW + L],
                                            bank[(1, 7)[b % 2]][:, 0:TB * G * L].rearrange("p (j g l) -> p j g l", j=TB, g=G),
                                            store[:, :, :, 0:L], ALU.subtract).then_inc(v_kept, 1)
                b = s - 1
                if live(b, looped):
                    c = b % CYC
                    dve.wait_ge(rstd_ok, b + o + 1)
                    if b >= CYC:
                        dve.wait_ge(xb_ok, b + o - CYC + 1)
                        dve.wait_ge(xT_ps, b + o - CYC + 1)
                    for j in range(TB):
                        last = nc.vector.tensor_scalar(xn[:, c, j, :], x_in[:, c, j, :], mv[:, c, j, 0:1], rstd[:, c, j:j + 1],
                                                       ALU.subtract, ALU.mult)
                    last.then_inc(xn_ok, 1)

            nc.vector.memset(ones_row[:, :], 1.0)
            nc.vector.memset(v_all[:, :, :, :, L:VW], 1.0)
            nc.vector.memset(v_all[:, :, :, :, VP - 1:VP], 0.0)
            nc.vector.memset(k_stack[KR:KM, :, :, :].bitcast(f32), 1.0).then_inc(dve_const, 1)
            dve.wait_ge(ld_router, 80)
            nc.vector.bn_stats(st_last, xlast).then_inc(last_step, 1)
            dve.wait_ge(last_step, 1)
            nc.vector.bn_aggr(mv_last, st_last).then_inc(last_step, 1)
            dve.wait_ge(last_step, 4)
            nc.vector.tensor_scalar(xnlast, xlast, mv_last[:, 0:1], rs_last, ALU.subtract, ALU.mult).then_inc(last_step, 1)
            dve.wait_ge(last_T, 1)
            nc.vector.tensor_copy(lastT, bank[6][:, 32:32 + B]).then_inc(last_cp, 1)
            dve.wait_ge(small_T, 1)
            nc.vector.tensor_copy(wupT, bank[7][:, 32:96].rearrange("p (k l) -> p k l", k=2))
            nc.vector.tensor_copy(b2rep, bank[7][:, 96:96 + E, None].to_broadcast([128, E, 128]))
            nc.vector.tensor_copy(table[:, :, B1_AT:B1_AT + FB],
                                  bank[7][:, 104:104 + E * FB].rearrange("p (f e) -> p e f", f=FB)).then_inc(tab_cp, 1)
            dve.wait_ge(lg_ps, 1)
            nc.vector.tensor_copy(logits, bank[6][0:B, 64:64 + E]).then_inc(sel_step, 1)
            dve.wait_ge(sel_step, 1)
            nc.vector.max(top8, logits).then_inc(sel_step, 1)
            dve.wait_ge(sel_step, 2)
            nc.vector.max_index(sel_idx[:, :], top8, logits).then_inc(sel_step, 1)
            dve.wait_ge(sel_step, 3)
            nc.vector.tensor_copy(selF, sel_idx[:, 0:1]).then_inc(sel_step, 1)
            dve.wait_ge(selT_ps, 1)
            nc.vector.tensor_copy(sel_row[:, :], bank[6][0:1, 96:96 + B]).then_inc(sel_ready, 1)
            step1(0, 0, 0, False)
            dve.wait_ge(wvT_ps, 1)
            wvT = bank[7][:, 0:G * 128].rearrange("p (g d) -> p g d", g=G)
            nc.vector.tensor_reduce(col_max, wvT, AX.X, ALU.max, apply_absolute_value=True).then_inc(wv_step, 1)
            dve.wait_ge(wv_step, 1)
            nc.vector.tensor_scalar(col_max, col_max, 1e-30, None, ALU.max).then_inc(wv_step, 1)
            dve.wait_ge(wv_step, 2)
            nc.vector.reciprocal(col_rcp, col_max).then_inc(wv_step, 1)
            dve.wait_ge(wv_step, 3)
            for g in range(G):
                last = nc.vector.tensor_scalar(wvdT[:, g, :], wvT[0:L, g, :], col_rcp[0:L, g:g + 1], None, ALU.mult)
            last.then_inc(wv_step, 1)
            step1(1, 0, 0, False)
            dve.wait_ge(wvd_ps, 1)
            nc.vector.tensor_copy(wvd[:, :], bank[7][:, 256:256 + G * L]).then_inc(wvd_ok, 1)
            dve.wait_ge(U_ps, 1)
            for g in range(G):
                last = nc.vector.tensor_scalar(U[:, g, :], bank[1][:, D * g:D * g + D], col_max[:, g:g + 1], 0.5, ALU.mult, ALU.mult)
            last.then_inc(U_cp, 1)
            step1(2, 0, 0, False)
            for i in range(2):
                dve.wait_ge(b2o_ps, i + 1)
                nc.vector.tensor_scalar(table[:, 4 * i:4 * i + 4, B2O_AT:B2O_AT + D],
                                        bank[6 + i][:, :].rearrange("p (e o) -> p e o", e=4), 0.3, None, ALU.mult).then_inc(tab_cp, 1)

            run(dve, step1, LAGS1, FIRST1, begun=3, left=JOINED)

            def step2(s, o, w, looped):
                def remainder(b, t):
                    if b >= 2:
                        dve.wait_ge(pv_ps, H * TB * (b + o - 1))
                    dve.wait_ge(p_hi_ok, PU * (b + o) + t + 1)
                    nc.vector.tensor_tensor(p_lo[:, b % 2, t, :], probs[:, t, :], p_hi[:, b % 2, t, :], ALU.subtract).then_inc(lo_dve, 1)

                def maxima(b, u):
                    blk, pair = u // 4, PAIRS[u % 4]
                    if u == 0 and b >= 2:
                        dve.wait_ge(mT_ps, b + o - 1)
                    dve.wait_ge(s_ps, SU * (b + o) + u + 1)
                    keys = 128 * (blk + 1)
                    nc.vector.tensor_reduce(neg_max[:, b % 2, blk, 2 * pair:2 * pair + 2],
                                            bank[2 + u % 2][:, :].rearrange("p (h k) -> p h k", h=2)[:, :, 0:keys],
                                            AX.X, ALU.max, negate=True).then_inc(max_ok, 1)

                def divide(b):
                    dve.wait_ge(pv_ps, H * TB * (b + o + 1))
                    if b >= 2:
                        dve.wait_ge(yT_ps, b + o - 1)
                    y = [bank[at][:, 0:H * VW].rearrange("p (h w) -> p h w", h=H) for at in (1, 6)]
                    for blk in range(TB):
                        last = nc.vector.reciprocal(rden[:, b % 2, blk, :], y[blk][:, :, L])
                    last.then_inc(rden_ok, 1)
                    dve.wait_ge(rden_ok, b + o + 1)
                    for blk in range(TB):
                        nc.vector.tensor_tensor(yn[:, b % 2, blk, :, :], y[blk][:, :, 0:L],
                                                rden[:, b % 2, blk, :, None].to_broadcast([128, H, L]), ALU.mult).then_inc(yn_ok, 1)

                for u in range(SU):
                    if live(s - 3, looped):
                        maxima(s - 3, u)
                    if u == 0 and live(s - 6, looped):
                        divide(s - 6)
                    b = s
                    if u == 3 and live(b, looped):
                        if b >= CYC:
                            for done in q_stacked[b % CYC // 2]:
                                dve.wait_ge(done, Q_STACK_DMAS * uses(b, w, CYC))
                        dve.wait_ge(q_hi_ok, b + o + 1)
                        nc.vector.tensor_tensor(q_lo[:, b % CYC, :, :], bank[0][:, :].rearrange("p (g t) -> p g t", g=G),
                                                q_hi[:, b % CYC, :, :].bitcast(f32), ALU.subtract).then_inc(q_lo_ok, 1)
                    if u in (1, 2, 4) and live(s - 5, looped):
                        remainder(s - 5, {1: 0, 2: 1, 4: 3}[u])
                    b = s
                    if u == 7 and live(b, looped):
                        c = k_buf(b)
                        dve.wait_ge(k_hi_ok, b + o + 1)
                        nc.vector.tensor_tensor(k_parts[:, 1, c, :], bank[0][0:G * L, 0:T], k_parts[:, 0, c, :].bitcast(f32),
                                                ALU.subtract).then_inc(k_lo_ok, 1)
                    b = s - 7
                    if u == 2 and live(b, looped):
                        dve.wait_ge(s_out, b + o + 1)
                        if b >= 2:
                            dve.wait_ge(res_ok, b + o - 1)
                        nc.vector.tensor_tensor(sg[:, b % 2, :, :], bank[7][:, 0:TB * D].rearrange("p (j d) -> p j d", j=TB),
                                                gate_all[:, bass.ds(b + o, 1), :, :].rearrange("p o j d -> p (o j) d"),
                                                ALU.mult).then_inc(sg_ok, 1)

            join(step1, step2)
            run(dve, step2, LAGS2, FIRST2, begun=JOINED)

        @block.tensor
        def _(pe):
            mm, tr = nc.tensor.matmul, nc.tensor.transpose
            def step1(s, o, w, looped):
                b = s - 3
                if live(b, looped):
                    c = b % CYC
                    pe.wait_ge(xT_ok, b + o + 1)
                    if b >= 2:
                        pe.wait_ge(v_kept, b + o - 1)
                    for j in range(TB):
                        last = mm(bank[(1, 7)[b % 2]][:, G * L * j:G * L * (j + 1)], xT[:, b % 2, 128 * j:128 * j + 128], wvd[:, :],
                                  start=True, stop=True)
                    last.then_inc(v_ps, 1)
                    pe.wait_ge(wsel_ld[c], 16 * (uses(b, w, CYC) + 1))
                    if b >= 2:
                        pe.wait_ge(h_ok, b + o - 1)
                    for f in range(FB):
                        last = mm(bank[2 + b % 2][:, T * f:T * f + T], wsel[:, c, W1_AT + 128 * f:W1_AT + 128 * f + 128], xT[:, b % 2, :],
                                  start=True, stop=True)
                    last.then_inc(h_ps, 1)
                b = s - 2
                if live(b, looped):
                    pe.wait_ge(xn_ok, b + o + 1)
                    if b >= 2:
                        pe.wait_ge(xT_ok, b + o - 1)
                    for j in range(TB):
                        last = tr(bank[(0, 6)[b % 2]][:, 128 * j:128 * j + 128], xn[:, b % CYC, j, :], ident[:, :])
                    last.then_inc(xT_ps, 1)
                b = s - 4
                if live(b, looped):
                    pe.wait_ge(h_ok, b + o + 1)
                    if b >= 2:
                        pe.wait_ge(z_ok, b + o - 1)
                    for j in range(TB):
                        for f in range(FB):
                            last = mm(bank[4 + b % 2][:, D * j:D * j + D], hT[:, b % 2, f, 128 * j:128 * j + 128],
                                      wsel[:, b % CYC, W2O_AT + D * f:W2O_AT + D * f + D], start=(f == 0), stop=(f == FB - 1))
                    last.then_inc(f2_ps, 1)

            pe.wait_ge(pool_const, 2)
            pe.wait_ge(ld_small, 64)
            tr(bank[7][:, 32:64], wup[:, 0, :], ident[0:L, 0:L])
            tr(bank[7][:, 64:96], wup[:, 1, :], ident[0:L, 0:L])
            tr(bank[7][:, 96:96 + E], b2_sb, ident[0:E, 0:E])
            for f in range(FB):
                last = tr(bank[7][:, 104 + E * f:104 + E * f + E], b1_sb[:, 128 * f:128 * f + 128], ident[0:E, 0:E])
            last.then_inc(small_T, 1)
            pe.wait_ge(last_step, 5)
            tr(bank[6][:, 32:32 + B], xnlast, ident[0:B, 0:B]).then_inc(last_T, 1)
            pe.wait_ge(last_cp, 1)
            mm(bank[6][:, 0:B], Wp1_sb, lastT, start=True, stop=True).then_inc(nav_ps, 1)
            pe.wait_ge(ld_wq, 16)
            for h in range(H):
                last = tr(bank[h // 4][:, 128 * (h % 4):128 * (h % 4) + 128], wq_sb[:, h, :], ident[:, :])
                if h % 4 == 3:
                    last.then_inc(wqT_ps, 1)
            pe.wait_ge(dve_const, 1)
            pe.wait_ge(nav_cp, 1)
            mm(bank[6][0:B, 64:64 + E], navT, Wp2_sb, start=True, stop=False)
            mm(bank[6][0:B, 64:64 + E], ones_row[:, 0:B], bp2_sb, start=False, stop=True).then_inc(lg_ps, 1)
            pe.wait_ge(ld_w2, 16)
            for i in range(E * FB):
                last = tr(bank[2 + i // 4][:, 128 * (i % 4):128 * (i % 4) + 128], W2_sb[:, i // FB, i % FB, :], ident[:, :])
                if i % 4 == 3:
                    last.then_inc(w2T_ps, 1)
            pe.wait_ge(sel_step, 4)
            mm(bank[6][0:1, 96:96 + B], selF, ident[0:B, 0:B], start=True, stop=True).then_inc(selT_ps, 1)
            pe.wait_ge(wqT_cp, 2)
            pe.wait_ge(tab_cp, 1)
            for h in range(H):
                last = mm(bank[0][:, L * h:L * h + L], wqT[:, h, :], wupT[:, 0, :], start=True, stop=True)
            last.then_inc(A_ps, 1)
            pe.wait_ge(ld_wo, 48)
            for h in range(H):
                r, g = h % R, h // R
                last = mm(bank[1][L * r:L * r + L, D * g:D * g + D], wupT[:, 1, :], wo_sb[:, h, :], start=True, stop=True)
            last.then_inc(U_ps, 1)
            pe.wait_ge(rep_ok, 1)
            for g in range(G):
                last = tr(bank[7][:, 128 * g:128 * g + 128], wvd_rep[:, g, :, :].rearrange("p r l -> p (r l)"), ident[:, :])
            last.then_inc(wvT_ps, 1)
            for i in range(E * FB):
                if i % 4 == 0:
                    pe.wait_ge(w2T_cp, i // 4 + 1)
                last = mm(bank[2 + i // 4][:, 128 * (i % 4):128 * (i % 4) + 128], W2T[:, i // FB, i % FB, :], Wo_sb, start=True, stop=True)
                if i % 4 == 3:
                    last.then_inc(w2o_ps, 1)
            pe.wait_ge(wv_step, 4)
            for g in range(G):
                last = tr(bank[7][:, 256 + L * g:256 + L * g + L], wvdT[:, g, :], ident[0:L, 0:L])
            last.then_inc(wvd_ps, 1)
            pe.wait_ge(A_cp, 1)
            step1(2, 0, 0, False)
            pe.wait_ge(wvd_ok, 1)
            pe.wait_ge(sel_ready, 1)
            for e in range(E):
                at = bank[6 + e // 4][:, 128 * (e % 4):128 * (e % 4) + 128]
                mm(at, b2rep[:, e, :], Wo_sb, start=True, stop=False)
                last = mm(at, ones_row[:, :], bo_sb, start=False, stop=True)
                if e % 4 == 3:
                    last.then_inc(b2o_ps, 1)
            pe.wait_ge(U_cp, 1)
            pe.wait_ge(tab_cp, 7)
            pe.wait_ge(ld_w1, 32)

            run(pe, step1, LAGS1, FIRST1, begun=3, left=JOINED)

            def step2(s, o, w, looped):
                def xnT(b):
                    return xnT_all[:, bass.ds(b + o, 1), :].rearrange("p o t -> p (o t)")

                def keys(b):
                    made = count(pe, b + o + 1, looped)
                    pe.wait_ge(pool_const, 2)
                    pe.wait_ge(q_lo_ok, made)
                    mm(bank[0][0:G * L, 0:T], wkd[:, :], xnT(b), start=True, stop=True).then_inc(k_ps, 1)

                def queries(b):
                    if b >= 4:
                        pe.wait_ge(m_row_ok, b + o - 3)
                    elif b >= 1:
                        pe.wait_ge(k_lo_ok, b)
                    else:
                        pe.wait_ge(xT_kept, B - 1)
                    for g in range(G):
                        last = mm(bank[0][:, T * g:T * g + T], A[:, 128 * g:128 * g + 128], xnT(b), start=True, stop=True)
                    last.then_inc(q_ps, 1)

                def transposed(b):
                    pe.wait_ge(yn_ok, TB * (b + o + 1))
                    if b >= 1:
                        pe.wait_ge(sg_ok, b + o)
                    for g in range(G):
                        for j in range(TB):
                            last = tr(bank[7][:, T * g + 128 * j:T * g + 128 * j + 128],
                                      yn[:, b % 2, j, R * g:R * g + R, :].rearrange("p h l -> p (h l)"), ident[:, :])
                    last.then_inc(yT_ps, 1)

                def projected(b):
                    pe.wait_ge(yT_ok, b + o + 1)
                    for j in range(TB):
                        for g in range(G):
                            last = mm(bank[7][:, D * j:D * j + D], yT[:, g, 128 * j:128 * j + 128], U[:, g, :], start=(g == 0), stop=(g == G - 1))
                    last.then_inc(s_out, 1)

                def scores(b, u):
                    c, blk, pair = b % CYC, u // 4, PAIRS[u % 4]
                    kc = k_buf(b)
                    if u in (0, 2):
                        pe.wait_ge(q_stacked[c // 2][pair % 2], Q_STACK_DMAS * (uses(b, w, CYC) + 1))
                    if u == 0:
                        pe.wait_ge(k_stacked[kc // 2], K_STACK_DMAS * (uses(b + 1, w, CYC) + 1))
                    if b == 0 and u == 0:
                        pe.wait_ge(h_ok, B)
                    if SU * b + u >= 2:
                        pe.wait_ge(max_ok, SU * (b + o) + u - 1)
                    at = bank[2 + u % 2]
                    for i in range(2):
                        h = 2 * pair + i
                        mm(at[:, T * i:T * i + T], q_stack[0:KR, h % R, c, h // R, 128 * blk:128 * blk + 128], k_stack[0:KR, h // R, kc, :],
                           start=(i == 0), stop=False)
                    mm(at[:, :].rearrange("p (h k) -> p h k", h=2)[:, :, 128 * blk:128 * blk + 128], identb[:, :], causal[:, :, :],
                       start=False, stop=True).then_inc(s_ps, 1)

                def maxima_by_head(b):
                    pe.wait_ge(max_ok, SU * (b + o + 1))
                    if looped or b + 3 < B:
                        pe.wait_ge(k_lo_ok, b + o + 4)
                    if b >= 1:
                        pe.wait_ge(m_row_ok, b + o)
                    for j in range(TB):
                        last = tr(bank[0][0:H, 128 * j:128 * j + 128], neg_max[:, b % 2, j, :], ident[:, :])
                    last.then_inc(mT_ps, 1)

                def shifted(b, t):
                    c, g, part = b % CYC, t // 3, t % 3
                    if part == 0:
                        pe.wait_ge(m_stacked[b % 2][g], 16 * (uses(b, w, 2) + 1))
                    if b == 0 and t == 0:
                        pe.wait_ge(z_ok, B)
                    if PU * b + t >= 2:
                        pe.wait_ge(exp_ok, PU * (b + o) + t - 1)
                    kb = part // 2
                    if kb == 0:
                        q = q_stack[0:KM, 2 * part:2 * part + 2, c, g, :]
                    else:
                        q = q_stack[0:KM, :, c, g, 128:256]
                    mm(bank[4 + t % 2][:, :], k_stack[0:KM, g, k_buf(b), 128 * kb:128 * kb + 128], q, start=True, stop=True).then_inc(st_ps, 1)

                def weighted(b, blk, h):
                    c, g, r = b % 2, h // R, h % R
                    if g == 0 and r == 0:
                        if blk == 0:
                            pe.wait_ge(vw_ld[b % CYC // 2], 16 * (uses(b, w, CYC) + 1))
                        if b >= 1:
                            pe.wait_ge(yn_ok, TB * (b + o) - 1 + blk)
                        elif blk == 0:
                            pe.wait_ge(v_kept, B)
                    if r % 2 == 0 and (blk == 0 or r == 0):
                        done, n = remainder_of(3 * g + (r // 2 if blk == 0 else 2))
                        pe.wait_ge(done, 3 * (b + o) + n)
                    at = bank[(1, 6)[blk]][:, VW * h:VW * h + VW]
                    pieces = [(3 * g + r // 2, T * (r % 2) + 128 * blk, 0)]
                    if blk == 1:
                        pieces.append((3 * g + 2, 128 * r, 1))
                    for n, (t, off, kb) in enumerate(pieces):
                        v_lead, v_rest = v_w[:, b % CYC, kb, g, 0:VW], v_w[:, b % CYC, kb, g, VW:VW + L]
                        hi, lo = p_hi[:, c, t, off:off + 128], p_lo[:, c, t, off:off + 128]
                        mm(at, hi, v_lead, start=(n == 0), stop=False)
                        mm(at[:, 0:L], hi, v_rest, start=False, stop=False)
                        last = mm(at, lo, v_lead, start=False, stop=(n == len(pieces) - 1))
                    last.then_inc(pv_ps, 1)

                for u in range(SU):
                    if live(s - 3, looped):
                        scores(s - 3, u)
                    if u < 2 and live(s - 5, looped):
                        shifted(s - 5, u + 4)
                    if u == 0 and live(s - 4, looped):
                        maxima_by_head(s - 4)
                    if u == 1 and live(s - 7, looped):
                        projected(s - 7)
                    if u == 2 and live(s, looped):
                        queries(s)
                    if u >= 4 and live(s - 4, looped):
                        shifted(s - 4, u - 4)
                    if u == 6 and live(s - 6, looped):
                        transposed(s - 6)
                    if u in (4, 7) and live(s - 5, looped):
                        g = (4, 7).index(u)
                        for blk in range(TB):
                            for r in range(R):
                                weighted(s - 5, blk, R * g + r)
                    if u == 5 and live(s, looped):
                        keys(s)

            join(step1, step2)
            run(pe, step2, LAGS2, FIRST2, begun=JOINED)


_INS = ["L0_attn_x", "L0_attn_wq", "L0_attn_wk_down", "L0_attn_wv_down", "L0_attn_wk_up", "L0_attn_wv_up", "L0_attn_wo",
        "L0_ffn_Wp1", "L0_ffn_bp1", "L0_ffn_Wp2", "L0_ffn_bp2", "L0_ffn_W1", "L0_ffn_b1", "L0_ffn_W2", "L0_ffn_b2",
        "L0_ffn_Wo", "L0_ffn_bo"]


def kernel(**inputs):
    import concourse.bacc as bacc
    from concourse.bass_utils import run_bass_kernel_spmd

    nc = bacc.Bacc("TRN2", target_bir_lowering=False, num_devices=1)
    arrays, args = {}, []
    for name in _INS:
        a = np.ascontiguousarray(inputs[name])
        arrays[name] = a
        args.append(nc.dram_tensor(name, a.shape, mybir.dt.from_np(a.dtype), kind="ExternalInput").ap())
    shape = arrays["L0_attn_x"].shape
    args.append(nc.dram_tensor("out", shape, mybir.dt.float32, kind="ExternalOutput").ap())
    layernorm_mla_attention_times_routed_ffn_gate(nc, *args)
    return run_bass_kernel_spmd(nc, [arrays], core_ids=[0]).results[0]["out"]
```
